# Optimizing a Trainium2 kernel written in Bass

```python
import numpy as np
import jax
import jax.numpy as jnp

def _softmax(x, axis=-1):
    return jax.nn.softmax(x, axis=axis)

def _gelu(x):
    return jax.nn.gelu(x, approximate=True)

def _silu(x):
    return jax.nn.silu(x)

def _sigmoid(x):
    return jax.nn.sigmoid(x)

def _layernorm(x, axis=-1, eps=1e-05):
    m = jnp.mean(x, axis=axis, keepdims=True)
    v = jnp.var(x, axis=axis, keepdims=True)
    return (x - m) / jnp.sqrt(v + eps)

def _scatter_add(tgt, idx, src, axis=0):
    return tgt.at[idx].add(src)

def _segment_sum(src, seg, n):
    return jax.ops.segment_sum(src, seg, n)
kernel_name = 'mk_seq_preln_d1_jaxref_r2_58f5d5'

def setup_inputs(seed: int=0):
    np.random.seed(seed)
    _w = jnp.asarray

    def _L0_attn_setup():
        import jax, jax.numpy as jnp
        import numpy as np
        import math
        HIDDEN = 1024
        NUM_HEADS = 16
        HEAD_DIM = HIDDEN // NUM_HEADS
        BATCH = 2
        SEQ = 2048
        BLOCK = 128
        TOPK = 64
        NEG = -1000000000.0

        def _split_heads(x):
            n, t, _ = x.shape
            return x.reshape(n, t, NUM_HEADS, HEAD_DIM).transpose(0, 2, 1, 3)

        def _local_attention(q, k, v):
            n, h, t, d = q.shape
            nb = t // BLOCK
            half = BLOCK // 2
            qb = q.reshape(n, h, nb, BLOCK, d)
            win = jnp.arange(nb)[:, None] * BLOCK - half + jnp.arange(2 * BLOCK)[None, :]
            valid = (win >= 0) & (win < t)
            winc = jnp.clip(win, 0, t - 1)
            kb = k[:, :, winc, :]
            vb = v[:, :, winc, :]
            scores = jnp.einsum('nhbqd,nhbkd->nhbqk', qb, kb) / math.sqrt(d)
            scores = jnp.where(valid[None, None, :, None, :], scores, NEG)
            probs = jax.nn.softmax(scores, axis=-1)
            ctx = jnp.einsum('nhbqk,nhbkd->nhbqd', probs, vb)
            return ctx.reshape(n, h, t, d)

        def _global_index(q):
            n, h, t, d = q.shape
            norm = jnp.linalg.norm(q, axis=-1)
            _, top_idx = jax.lax.top_k(norm, TOPK - 2)
            bos = jnp.zeros((n, h, 1), jnp.int32)
            eos = jnp.full((n, h, 1), t - 1, jnp.int32)
            return jnp.concatenate([bos, top_idx.astype(jnp.int32), eos], axis=-1)
        key = jax.random.key(seed)
        ks = jax.random.split(key, 7)
        s = 1.0 / math.sqrt(HIDDEN)
        return {'hidden_states': jax.random.normal(ks[0], (BATCH, SEQ, HIDDEN), jnp.float32), 'Wq': jax.random.normal(ks[1], (HIDDEN, HIDDEN), jnp.float32) * s, 'bq': jnp.zeros((HIDDEN,), jnp.float32), 'Wk': jax.random.normal(ks[2], (HIDDEN, HIDDEN), jnp.float32) * s, 'bk': jnp.zeros((HIDDEN,), jnp.float32), 'Wv': jax.random.normal(ks[3], (HIDDEN, HIDDEN), jnp.float32) * s, 'bv': jnp.zeros((HIDDEN,), jnp.float32)}
    _L0_attn_in = _L0_attn_setup()

    def _L0_ffn_setup():
        import jax, jax.numpy as jnp
        import numpy as np
        key = jax.random.key(seed)
        k1, k2, k3, k4 = jax.random.split(key, 4)
        B, S, D_IN, D_OUT = (4, 2048, 1024, 1024)
        x = jax.random.normal(k1, (B, S, D_IN), dtype=jnp.float32)
        weight = jax.random.normal(k2, (D_OUT, D_IN), dtype=jnp.float32) * 0.02
        scale_weight = jax.random.uniform(k3, (D_OUT,), dtype=jnp.float32, minval=0.5, maxval=1.5)
        bias = jax.random.normal(k4, (D_OUT,), dtype=jnp.float32) * 0.02
        return {'x': x, 'weight': weight, 'scale_weight': scale_weight, 'bias': bias}
    _L0_ffn_in = _L0_ffn_setup()
    _d = {'L0_attn_hidden_states': _L0_attn_in['hidden_states'], 'L0_attn_Wq': _L0_attn_in['Wq'], 'L0_attn_bq': _L0_attn_in['bq'], 'L0_attn_Wk': _L0_attn_in['Wk'], 'L0_attn_bk': _L0_attn_in['bk'], 'L0_attn_Wv': _L0_attn_in['Wv'], 'L0_attn_bv': _L0_attn_in['bv'], 'L0_ffn_weight': _L0_ffn_in['weight'], 'L0_ffn_scale_weight': _L0_ffn_in['scale_weight'], 'L0_ffn_bias': _L0_ffn_in['bias']}
    _x0 = _d['L0_attn_hidden_states']
    _d['L0_attn_hidden_states'] = jax.random.normal(jax.random.fold_in(jax.random.key(seed), 1), (4, 1024, 1024), dtype=_x0.dtype)
    del _x0
    return _d

def reference(L0_attn_hidden_states, L0_attn_Wq, L0_attn_bq, L0_attn_Wk, L0_attn_bk, L0_attn_Wv, L0_attn_bv, L0_ffn_weight, L0_ffn_scale_weight, L0_ffn_bias):

    def _L0_attn_ref(hidden_states, Wq, bq, Wk, bk, Wv, bv):
        import jax, jax.numpy as jnp
        import numpy as np
        import math
        HIDDEN = 1024
        NUM_HEADS = 16
        HEAD_DIM = HIDDEN // NUM_HEADS
        BATCH = 2
        SEQ = 2048
        BLOCK = 128
        TOPK = 64
        NEG = -1000000000.0

        def _split_heads(x):
            n, t, _ = x.shape
            return x.reshape(n, t, NUM_HEADS, HEAD_DIM).transpose(0, 2, 1, 3)

        def _local_attention(q, k, v):
            n, h, t, d = q.shape
            nb = t // BLOCK
            half = BLOCK // 2
            qb = q.reshape(n, h, nb, BLOCK, d)
            win = jnp.arange(nb)[:, None] * BLOCK - half + jnp.arange(2 * BLOCK)[None, :]
            valid = (win >= 0) & (win < t)
            winc = jnp.clip(win, 0, t - 1)
            kb = k[:, :, winc, :]
            vb = v[:, :, winc, :]
            scores = jnp.einsum('nhbqd,nhbkd->nhbqk', qb, kb) / math.sqrt(d)
            scores = jnp.where(valid[None, None, :, None, :], scores, NEG)
            probs = jax.nn.softmax(scores, axis=-1)
            ctx = jnp.einsum('nhbqk,nhbkd->nhbqd', probs, vb)
            return ctx.reshape(n, h, t, d)

        def _global_index(q):
            n, h, t, d = q.shape
            norm = jnp.linalg.norm(q, axis=-1)
            _, top_idx = jax.lax.top_k(norm, TOPK - 2)
            bos = jnp.zeros((n, h, 1), jnp.int32)
            eos = jnp.full((n, h, 1), t - 1, jnp.int32)
            return jnp.concatenate([bos, top_idx.astype(jnp.int32), eos], axis=-1)
        q = _split_heads(hidden_states @ Wq + bq)
        k = _split_heads(hidden_states @ Wk + bk)
        v = _split_heads(hidden_states @ Wv + bv)
        n, h, t, d = q.shape
        ctx = _local_attention(q, k, v)
        idx = _global_index(q)
        qg = jnp.take_along_axis(q, idx[..., None], axis=-2)
        g_scores = jnp.einsum('nhqd,nhkd->nhqk', qg, k) / math.sqrt(d)
        g_probs = jax.nn.softmax(g_scores, axis=-1)
        g_ctx = jnp.einsum('nhqk,nhkd->nhqd', g_probs, v)
        bn = jnp.arange(n)[:, None, None]
        bh = jnp.arange(h)[None, :, None]
        ctx = ctx.at[bn, bh, idx].set(g_ctx)
        out = ctx.transpose(0, 2, 1, 3).reshape(n, t, h * d)
        return out

    def _L0_ffn_ref(x, weight, scale_weight, bias):
        import jax, jax.numpy as jnp
        import numpy as np
        w = weight * scale_weight[:, None]
        out = jnp.einsum('bsi,oi->bso', x, w) + bias
        return out
    x = L0_attn_hidden_states
    x = x + _L0_attn_ref(_layernorm(x, axis=-1), L0_attn_Wq, L0_attn_bq, L0_attn_Wk, L0_attn_bk, L0_attn_Wv, L0_attn_bv)
    x = x + _L0_ffn_ref(_layernorm(x, axis=-1), L0_ffn_weight, L0_ffn_scale_weight, L0_ffn_bias)
    return x

_drawn_inputs = setup_inputs


def setup_inputs(seed=0):
    import zlib

    import numpy as np

    out = dict(_drawn_inputs(seed))
    spreads = {'L0_attn_bq': (0.0, 0.531), 'L0_attn_bk': (0.0, 0.8), 'L0_attn_bv': (0.0, 0.1)}
    factors = {'L0_ffn_bias': 3.761}
    for name, (base, spread) in spreads.items():
        noise = np.random.default_rng([zlib.crc32(name.encode()), seed]).standard_normal(out[name].shape)
        drawn = base * np.exp(spread * noise) if base else spread * noise
        out[name] = jnp.asarray(drawn.astype(out[name].dtype))
    for name, factor in factors.items():
        out[name] = (out[name] * factor).astype(out[name].dtype)
    return out
```

```python
from contextlib import ExitStack

import concourse.bass as bass
from concourse import mybir

F32 = mybir.dt.float32
F32R = mybir.dt.float32r
U32 = mybir.dt.uint32
ALU = mybir.AluOpType
ACT = mybir.ActivationFunctionType
AX = mybir.AxisListType

P = 128
BATCH, SEQ, HID, HEADS = 4, 1024, 1024, 16
HD = HID // HEADS
PAIRS = HEADS // 2
KC = HID // P
TILES = SEQ // P
HALF = 512
BLK = 128
STEPS = SEQ // (2 * BLK)
TOPK = 64
EPS = 1e-5
SLICES = 3 * PAIRS
BUFS = SLICES // 2
EVENTS = STEPS + 1
MISC = 4
LN_LINKS = 6
SKIP = float(1 << 20)
ROWS = BATCH * SEQ * HEADS
TOKENS = BATCH * SEQ
OUT_TILES = TOKENS // P
TOP_LINKS = 2 * (TOPK // 8) + 6


def build(nc, x_in, wstream, bq, bk, bv, w_ffn, scale_ffn, bias_ffn, out):
    q_rows = nc.dram_tensor("q_rows", (SEQ * HEADS, HD), F32, kind="Internal").ap()
    ctx_rows = nc.dram_tensor("ctx_rows", (ROWS, HD), F32, kind="Internal").ap()
    idx_dram = nc.dram_tensor("idx_dram", (BATCH, 2 * HEADS * TOPK), U32, kind="Internal").ap()
    q_tiles = q_rows.rearrange("(t p h) d -> p t (h d)", p=P, h=HEADS)
    ctx_tiles = ctx_rows.rearrange("(t p h) d -> p t (h d)", p=P, h=HEADS)
    x_tiles = x_in.rearrange("n (t p) c -> (n t) p c", p=P)
    out_tiles = out.rearrange("n (t p) c -> (n t) p c", p=P)
    w_tiles = w_ffn.rearrange("(t p) c -> t p c", p=P)

    with ExitStack() as ctx:
        def sb(name, shape, dt=F32):
            return ctx.enter_context(nc.sbuf_tensor(name, shape, dt))

        def sem(name):
            return ctx.enter_context(nc.semaphore(name))

        xT_hi, xT_lo = sb("xT_hi", [P, KC, SEQ], F32R), sb("xT_lo", [P, KC, SEQ], F32R)
        q_store = sb("q_store", [P, PAIRS, SEQ])
        w_raw = [sb(f"w_raw{b}", [P, KC * P]) for b in range(2)]
        w_hi = [sb(f"w_hi{b}", [P, KC * P], F32R) for b in range(2)]
        w_lo = [sb(f"w_lo{b}", [P, KC * P], F32R) for b in range(2)]
        qT_cur = sb("qT_cur", [P, SEQ])
        q_nat = sb("q_nat", [P, TILES, P])
        q_sq = sb("q_sq", [P, SEQ // 2])
        qT_hi, qT_lo = sb("qT_hi", [P, SEQ], F32R), sb("qT_lo", [P, SEQ], F32R)
        kT_hi, kT_lo = sb("kT_hi", [P, SEQ], F32R), sb("kT_lo", [P, SEQ], F32R)
        vT = sb("vT", [P, SEQ])
        v_nat = sb("v_nat", [P, TILES + 1, 2, P], F32R)
        probs = sb("probs", [P, SEQ])
        pT_hi, pT_lo = sb("pT_hi", [P, SEQ + P], F32R), sb("pT_lo", [P, SEQ + P], F32R)
        x_buf, x_norm = sb("x_buf", [P, 2, HID]), sb("x_norm", [P, 2, HID])
        ident = sb("ident", [P, P])
        bq_c, bk_c, bv_c = sb("bq_c", [P, PAIRS]), sb("bk_c", [P, PAIRS]), sb("bv_c", [P, PAIRS])
        scale_c = sb("scale_c", [P, KC])
        bias_b = sb("bias_b", [P, HID])
        ln_stats, ln_mv = sb("ln_stats", [P, 2, 6]), sb("ln_mv", [P, 2])
        ln_var, ln_std, ln_rec = sb("ln_var", [P, 1]), sb("ln_std", [P, 1]), sb("ln_rec", [P, 1])
        ln_two, ln_half, ln_rstd = sb("ln_two", [P, 1]), sb("ln_half", [P, 1]), sb("ln_rstd", [P, 1])
        norms = sb("norms", [P, TILES, HEADS])
        norm_rows = x_norm[0:HEADS, :, :]
        top_val = sb("top_val", [HEADS, 8])
        top_idx = sb("top_idx", [HEADS, TOPK], U32)
        idx_f = sb("idx_f", [HEADS, TOPK])
        idx_eq, idx_dup = sb("idx_eq", [HEADS, 2, TOPK - 2]), sb("idx_dup", [HEADS, 2])
        idx_row, idx_dst, idx_skip = (sb(name, [HEADS, TOPK]) for name in ("idx_row", "idx_dst", "idx_skip"))
        idx_out = sb("idx_out", [HEADS, 2, TOPK], U32)
        row_base, batch_base = sb("row_base", [HEADS, 1]), sb("batch_base", [HEADS, 1])
        idx_cols = sb("idx_cols", [P, 2, PAIRS], U32)
        q_sel = sb("q_sel", [P, PAIRS, HD])
        q_pad = sb("q_pad", [P, P])
        gq_hi, gq_lo = sb("gq_hi", [P, P], F32R), sb("gq_lo", [P, P], F32R)
        neg_max = sb("neg_max", [P, 4 * EVENTS])
        row_sum, row_inv = sb("row_sum", [P, 4 * EVENTS]), sb("row_inv", [P, 4 * EVENTS])
        pv_lo = sb("pv_lo", [P, 4, HD])
        pv_sum = sb("pv_sum", [P, 2, 4, HD])
        ctx_out = sb("ctx_out", [P, 2, 2, 2, HD])
        g_sum = sb("g_sum", [P, HD])
        g_ctx = sb("g_ctx", [P, PAIRS, HD])
        lin_c, lin_h = q_store[:, 0:2, :], q_store[:, 2:4, :]
        lin_hb, lin_o = q_store[:, 4:6, :], q_store[:, 6:8, :]
        xlT_hi, xlT_lo = [kT_hi, qT_hi], [kT_lo, qT_lo]

        proj = ctx.enter_context(nc.psum_tensor("proj", [P, 2, 512], F32))
        score = ctx.enter_context(nc.psum_tensor("score", [P, 1024], F32))
        turn = ctx.enter_context(nc.psum_tensor("turn", [P, 1024], F32))
        pv = ctx.enter_context(nc.psum_tensor("pv", [P, 512], F32))
        misc = ctx.enter_context(nc.psum_tensor("misc", [P, 512], F32))
        score4 = score[:, :].rearrange("p (g k) -> p g k", g=4)

        const_in = sem("const_in"); ident_zero = sem("ident_zero"); ident_set = sem("ident_set")
        base_set = sem("base_set"); pad_zero = sem("pad_zero")
        raw_in = [sem(f"raw_in{b}") for b in range(2)]
        w_hi_set = sem("w_hi_set")
        w_split = [sem(f"w_split{b}") for b in range(2)]
        x_in_s = [sem(f"x_in{b}") for b in range(2)]
        ln_step = sem("ln_step"); ln_var_set = sem("ln_var_set"); ln_std_set = sem("ln_std_set")
        xn_set = sem("xn_set"); ln_turned = sem("ln_turned"); xT_hi_set = sem("xT_hi_set"); xT_set = sem("xT_set")
        proj_done = [sem(f"proj_done{h}") for h in range(2)]
        proj_free = [sem(f"proj_free{h}") for h in range(2)]
        qT_set = [sem(f"qT_set{h}") for h in range(2)]
        q_turned = [sem(f"q_turned{h}") for h in range(2)]
        q_nat_set = [sem(f"q_nat_set{h}") for h in range(2)]
        q_squared = [sem(f"q_squared{h}") for h in range(2)]
        q_stored = [sem(f"q_stored{h}") for h in range(2)]
        norm_set = sem("norm_set"); norm_turned = sem("norm_turned"); norm_rows_set = sem("norm_rows_set")
        top_step = sem("top_step"); idx_set = sem("idx_set"); idx_dma = sem("idx_dma"); sel_in = sem("sel_in")
        qh_set = sem("qh_set"); q_split = sem("q_split")
        k_hi_set = [sem(f"k_hi_set{h}") for h in range(2)]
        scored = sem("scored"); max_set = sem("max_set"); exp_set = sem("exp_set")
        p_turned = sem("p_turned"); pT_hi_set = sem("pT_hi_set"); pT_set = sem("pT_set")
        m_turned = sem("m_turned"); m_hi_set = sem("m_hi_set"); m_set = sem("m_set")
        pad_set = sem("pad_set")
        pv_done = sem("pv_done"); pv_lo_set = sem("pv_lo_set")
        pv_free = sem("pv_free")
        inv_set = sem("inv_set")
        ctx_set = sem("ctx_set")
        ctx_stored = [sem(f"ctx_stored{b}") for b in range(2)]
        g_set = sem("g_set"); scattered = sem("scattered")
        h_set = sem("h_set"); hb_set = sem("hb_set"); lin_done = [sem(f"lin_done{h}") for h in range(2)]
        o_set = sem("o_set")
        o_stored = [sem(f"o_stored{b}") for b in range(2)]

        def window(i):
            lo, hi = max(0, i * BLK - BLK // 2), min(SEQ, (i + 1) * BLK + BLK // 2)
            return lo, hi, lo - (i * BLK - BLK // 2)

        def groups(s):
            if s == 0:
                return [(0, 64, 256), (1, 0, 256)]
            if s == STEPS - 1:
                return [(0, 0, 256), (1, 0, 192)]
            return [(None, 0, 256)]

        def turned_pieces(s):
            if s == 0:
                return [(64, 0, 128), (P, 128, 384)]
            if s == STEPS - 1:
                return [(P, 0, 384), (64, 384, 128)]
            return [(P, 0, 512)]

        def tile_tokens(j):
            return max(0, P * j - 64), min(SEQ, P * j + 64)

        V_GROUPS = [[(0, 0), (8, 128), (1, 256), (2, 384)], [(3, 0), (4, 128), (5, 256), (6, 384)], [(7, 0)]]
        V_PIECES = [[(64, 0, TILES, 2, 0), (P, 1, 1, 2, 256)], [(P, 3, 1, 4, 0)], [(P, 7, 1, 1, 0)]]

        passed = sem("passed")

        def apart(eng):
            eng.sem_inc(passed, 1)

        block = ctx.enter_context(nc.Block())

        @block.sync
        def _(sp):
            for b in range(2):
                sp.sem_inc(q_stored[b], 16)
                sp.sem_inc(o_stored[b], 16)
            for dst, src in ((bq_c, bq), (bk_c, bk), (bv_c, bv), (scale_c, scale_ffn)):
                sp.dma_start(dst[:, :], src).then_inc(const_in, 16)
            sp.dma_start(bias_b[:, :], bias_ffn.partition_broadcast(P)).then_inc(const_in, 16)

            def load_slice(n, i, b, count):
                sp.wait_ge(w_split[b], count + 1)
                sp.dma_start(w_raw[b][:, :], wstream[i]).then_inc(raw_in[b], 16)

            def store_ctx(n, hp, s):
                sp.wait_ge(ctx_set, n * (PAIRS * STEPS) + hp * STEPS + s + 1 + STEPS)
                sp.dma_start(ctx_tiles[:, bass.ds(n * TILES + 2 * s, 2), bass.ds(hp * P, P)],
                             ctx_out[:, s % 2].rearrange("p b h d -> p b (h d)")).then_inc(ctx_stored[s % 2], 16)

            with sp.Fori(0, BATCH) as n:
                for b in range(2):
                    load_slice(n, b, b, n * BUFS)
                for t in range(TILES):
                    if t >= 2:
                        sp.wait_ge(xn_set, n * TILES + t - 1)
                    sp.dma_start(x_buf[:, t % 2, :], x_tiles[n * TILES + t]).then_inc(x_in_s[t % 2], 16)
                with sp.Fori(0, PAIRS // 2) as j:
                    for b, h in ((0, 0), (0, 1), (1, 0), (1, 1)):
                        if h == 0:
                            load_slice(n, 2 * j + b + 2, b, n * BUFS + j + 1)
                        sp.wait_ge(q_nat_set[h], n * PAIRS + 2 * j + b + 1)
                        sp.dma_start(q_tiles[:, 4 * h:4 * h + 4, bass.ds((2 * j + b) * P, P)],
                                     q_nat[:, 4 * h:4 * h + 4, :]).then_inc(q_stored[h], 16)
                for b in range(2):
                    load_slice(n, PAIRS + 2 + b, b, n * BUFS + PAIRS // 2 + 1)
                with sp.Fori(0, PAIRS - 2) as hp:
                    load_slice(n, PAIRS + 4 + 2 * hp, 0, n * BUFS + PAIRS // 2 + 2 + hp)
                    store_ctx(n, hp, 0)
                    store_ctx(n, hp, 1)
                    load_slice(n, PAIRS + 5 + 2 * hp, 1, n * BUFS + PAIRS // 2 + 2 + hp)
                    store_ctx(n, hp, 2)
                    store_ctx(n, hp, 3)
                for hp in (PAIRS - 2, PAIRS - 1):
                    for s in range(STEPS):
                        store_ctx(n, hp, s)

            for t in range(TILES):
                if t >= 2:
                    sp.wait_ge(xn_set, BATCH * TILES + t - 1)
                sp.dma_start(x_buf[:, t % 2, :], w_tiles[t]).then_inc(x_in_s[t % 2], 16)
            for b in range(2):
                sp.wait_ge(ctx_stored[b], 16 + 16 * BATCH * PAIRS * STEPS // 2)
            sp.wait_ge(scattered, 16 * BATCH * PAIRS)
            LIN_XN = (BATCH + 1) * TILES

            def store_out(t, b):
                sp.wait_ge(o_set, 2 * t + 4)
                sp.dma_start(out_tiles[t], lin_o[:, b, :]).then_inc(o_stored[b], 16)

            def load_x(t, b):
                sp.dma_start(x_buf[:, b, :], x_tiles[t]).then_inc(x_in_s[b], 16)
                sp.dma_start(lin_c[:, b, :], ctx_tiles[:, t, :]).then_inc(x_in_s[b], 16)

            sp.wait_ge(xn_set, LIN_XN)
            load_x(0, 0)
            load_x(1, 1)
            with sp.Fori(0, OUT_TILES // 2 - 1) as j:
                for b in range(2):
                    sp.wait_ge(h_set, 2 * j + b + 1)
                    load_x(2 * j + 2 + b, b)
                    store_out(2 * j + b, b)
            for b in range(2):
                store_out(OUT_TILES - 2 + b, b)
            for b in range(2):
                sp.wait_ge(o_stored[b], 16 + 16 * OUT_TILES // 2)

        @block.gpsimd
        def _(pool):
            for b in range(2):
                pool.sem_inc(w_split[b], 1)
                pool.sem_inc(ctx_stored[b], 16)
            pool.sem_inc(ctx_set, STEPS)
            pool.memset(ident[:, :], 0.0).then_inc(ident_zero, 1)
            pool.wait_ge(ident_zero, 1)
            pool.affine_select(out=ident[:, :], in_=ident[:, :], compare_op=ALU.not_equal, fill=1.0, base=0,
                               pattern=[[-1, P]], channel_multiplier=1).then_inc(ident_set, 1)
            pool.iota(row_base[:, :], [[0, 1]], base=0, channel_multiplier=1,
                      allow_small_or_imprecise_dtypes=True).then_inc(base_set, 1)
            pool.memset(q_pad[:, :], 0.0).then_inc(pad_zero, 1)

            def split(n, i, b, count):
                pool.wait_ge(raw_in[b], 16 * count + 16)
                if not (isinstance(i, int) and i < 2):
                    pool.wait_ge(proj_done[1], n * SLICES + i - 1)
                apart(pool)
                pool.tensor_copy(w_hi[b][:, :], w_raw[b][:, :]).then_inc(w_hi_set, 1)
                pool.wait_ge(w_hi_set, n * SLICES + i + 1)
                pool.tensor_tensor(w_lo[b][:, :], w_raw[b][:, :], w_hi[b][:, :].bitcast(F32),
                                   ALU.subtract).then_inc(w_split[b], 1)

            def normalise(n, hp, s):
                u = n * PAIRS + hp
                pool.wait_ge(inv_set, u * EVENTS + s + 1)
                pool.wait_ge(pv_free, u * EVENTS + s + 2)
                pool.wait_ge(ctx_stored[s % 2], u * (16 * STEPS // 2) + 16 * (s // 2) + 16)
                pool.tensor_tensor(ctx_out[:, s % 2].rearrange("p b h d -> p h b d"),
                                   pv_sum[:, s % 2].rearrange("p (h b) d -> p h b d", h=2),
                                   row_inv[:, 4 * s:4 * s + 4].rearrange("p (h b) -> p h b", h=2).unsqueeze(3)
                                   .broadcast_to([P, 2, 2, HD]),
                                   ALU.mult).then_inc(ctx_set, 1)

            with pool.Fori(0, BATCH) as n:
                split(n, 0, 0, n * BUFS)
                split(n, 1, 1, n * BUFS)
                apart(pool)
                with pool.Fori(0, PAIRS // 2) as j:
                    for b in range(2):
                        split(n, 2 * j + b + 2, b, n * BUFS + j + 1)
                split(n, PAIRS + 2, 0, n * BUFS + PAIRS // 2 + 1)
                pool.wait_ge(idx_set, n * 2 + 2)
                apart(pool)
                pool.dma_start(idx_dram[n].rearrange("(g h s) -> h g s", g=2, s=TOPK),
                               idx_out[:, :, :]).then_inc(idx_dma, 16)
                pool.wait_ge(idx_dma, n * 48 + 16)
                apart(pool)
                for r in range(2):
                    src = idx_dram[n].rearrange("(e r s) -> r s e", r=2, s=TOPK)
                    pool.dma_start(idx_cols[r * TOPK:r * TOPK + TOPK, :, :].rearrange("p g e -> p (g e)"), src[r],
                                   allow_slow_non_contiguous=True).then_inc(idx_dma, 16)
                pool.wait_ge(idx_dma, n * 48 + 48)
                for h in range(2):
                    pool.wait_ge(q_stored[h], n * (16 * PAIRS) + 16 * PAIRS + 16)
                apart(pool)
                for hp in range(PAIRS):
                    pool.indirect_dma_start(q_sel[:, hp, :], None, q_rows,
                                            bass.IndirectOffsetOnAxis(ap=idx_cols[:, 0, hp:hp + 1], axis=0)
                                            ).then_inc(sel_in, 16)
                apart(pool)
                with pool.Fori(0, PAIRS - 2) as hp:
                    split(n, PAIRS + 3 + 2 * hp, 1, n * BUFS + PAIRS // 2 + 1 + hp)
                    normalise(n, hp, 0)
                    normalise(n, hp, 1)
                    split(n, PAIRS + 4 + 2 * hp, 0, n * BUFS + PAIRS // 2 + 2 + hp)
                    normalise(n, hp, 2)
                    normalise(n, hp, 3)
                split(n, SLICES - 1, 1, n * BUFS + BUFS - 1)
                for hp in (PAIRS - 2, PAIRS - 1):
                    for s in range(STEPS):
                        normalise(n, hp, s)
                for b in range(2):
                    pool.wait_ge(ctx_stored[b], (n + 1) * (16 * PAIRS * STEPS // 2) + 16)
                pool.wait_ge(g_set, n * PAIRS + PAIRS)
                apart(pool)
                for hp in range(PAIRS):
                    pool.indirect_dma_start(ctx_rows, bass.IndirectOffsetOnAxis(ap=idx_cols[:, 1, hp:hp + 1], axis=0),
                                            g_ctx[:, hp, :], None, bounds_check=ROWS - 1, oob_is_err=False
                                            ).then_inc(scattered, 16)
                pool.wait_ge(scattered, (n + 1) * (16 * PAIRS))

            pool.wait_ge(const_in, 80)

            def add_bias(t, b):
                pool.wait_ge(h_set, t + 1)
                pool.tensor_tensor(lin_hb[:, b, :], lin_h[:, b, :], bias_b[:, :], ALU.add).then_inc(hb_set, 1)

            add_bias(0, 0)
            add_bias(1, 1)
            with pool.Fori(1, OUT_TILES // 2) as j:
                for b in range(2):
                    pool.wait_ge(o_set, 4 * j + 2 * b)
                    add_bias(2 * j + b, b)

        @block.tensor
        def _(pe):
            pe.wait_ge(ident_set, 1)

            def project(b, half, part):
                terms = [(w, x, k) for w, x in ((w_hi, xT_hi), (w_lo, xT_hi), (w_hi, xT_lo)) for k in range(KC)]
                for m in range(12 * part, 12 * part + 12):
                    w, x, k = terms[m]
                    mm = pe.matmul(proj[:, half, :], w[b][:, k * P:k * P + P], x[:, k, half * HALF:half * HALF + HALF],
                                   start=(m == 0), stop=(m == 23), skip_group_check=True)
                return mm

            def project_half(n, i, b, count, half, parts=(0, 1)):
                for part in parts:
                    if part == 0:
                        if half == 0:
                            pe.wait_ge(w_split[b], count + 2)
                        pe.wait_ge(proj_free[half], n * SLICES + i + 1)
                    mm = project(b, half, part)
                    if part == 1:
                        mm.then_inc(proj_done[half], 1)

            def turn_q(n, hp, h):
                pe.wait_ge(qT_set[h], n * PAIRS + hp + 1)
                for t in range(4):
                    last = pe.transpose(turn[:, h * 512 + t * P:h * 512 + t * P + P],
                                        qT_cur[:, h * HALF + t * P:h * HALF + t * P + P], ident[:, :])
                last.then_inc(q_turned[h], 1)

            def scores(u, s, at_k):
                if s == 0:
                    pe.wait_ge(q_split, u + 1)
                if s < 2:
                    pe.wait_ge(proj_free[s], at_k + 2)
                for qs, ks, first, stop in ((qT_hi, kT_hi, True, False), (qT_lo, kT_hi, False, False),
                                            (qT_hi, kT_lo, False, True)):
                    for b in range(2):
                        i = 2 * s + b
                        lo, hi, col = window(i)
                        for h in range(2):
                            r = slice(h * HD, h * HD + HD)
                            at = h * 512 + b * 256 + col
                            mm = pe.matmul(score[:, at:at + hi - lo], qs[r, i * BLK:i * BLK + BLK], ks[r, lo:hi],
                                           start=(first and b == 0), stop=stop, skip_group_check=True)
                mm.then_inc(scored, 1)

            def turn_p(u, s):
                pe.wait_ge(exp_set, u * EVENTS + s + 1)
                if s == 0:
                    apart(pe)
                for h in range(2):
                    for b in range(2):
                        for c in range(2):
                            a, z = tile_tokens(2 * s + b + c)
                            rows = z - a
                            col = h * 512 + b * 256 + c * P
                            src = col + (64 if (rows < P and c == 0) else 0)
                            mm = pe.transpose(turn[0:rows, col:col + P], probs[:, src:src + rows], ident[:, :])
                mm.then_inc(p_turned, 1)

            def weigh(u, s):
                pe.wait_ge(pT_set, u * EVENTS + s + 1)
                pe.wait_ge(pv_free, u * EVENTS + s + 1)
                for h in range(2):
                    for b in range(2):
                        g = h * 2 + b
                        for m, (pt, c) in enumerate(((pT_hi, 0), (pT_hi, 1), (pT_lo, 0), (pT_lo, 1))):
                            a, z = tile_tokens(2 * s + b + c)
                            rows = z - a
                            mm = pe.matmul(pv[:, g * P:g * P + P], pt[0:rows, (g * 2 + c) * P:(g * 2 + c) * P + P],
                                           v_nat[0:rows, 2 * s + b + c, h, :], start=(m == 0), stop=(m == 3))
                mm.then_inc(pv_done, 1)

            def turn_v(u, g, at_v):
                if g == 0:
                    for h in range(2):
                        pe.wait_ge(proj_free[h], at_v + 2)
                else:
                    pe.wait_ge(m_set, u * MISC + g)
                apart(pe)
                for j, col in V_GROUPS[g]:
                    a, z = tile_tokens(j)
                    mm = pe.transpose(misc[0:z - a, col:col + P], vT[:, a:z], ident[:, :])
                mm.then_inc(m_turned, 1)

            def turn_gq(u):
                pe.wait_ge(m_set, u * MISC + 3)
                pe.wait_ge(pad_set, u + 1)
                pe.transpose(misc[:, 0:P], q_pad[:, :], ident[:, :]).then_inc(m_turned, 1)

            def global_scores(u):
                pe.wait_ge(m_set, u * MISC + 4)
                for qs, ks, first, stop in ((gq_hi, kT_hi, True, False), (gq_lo, kT_hi, False, False),
                                            (gq_hi, kT_lo, False, True)):
                    for h in range(2):
                        mm = pe.matmul(score[:, h * 512:h * 512 + 512], qs[:, :], ks[:, h * 512:h * 512 + 512],
                                       start=first, stop=stop, skip_group_check=True)
                mm.then_inc(scored, 1)

            def turn_gp(u):
                pe.wait_ge(exp_set, u * EVENTS + EVENTS)
                apart(pe)
                for j in range(TILES + 1):
                    a, z = tile_tokens(j)
                    dst = turn[0:z - a, (j - 1) * P:j * P] if 0 < j else misc[0:64, 0:P]
                    mm = pe.transpose(dst, probs[:, a:z], ident[:, :])
                mm.then_inc(p_turned, 1)

            def global_weigh(u):
                pe.wait_ge(pT_set, u * EVENTS + EVENTS)
                pe.wait_ge(pv_free, u * EVENTS + EVENTS)
                for m, pt in enumerate((pT_hi, pT_lo)):
                    for j in range(TILES + 1):
                        a, z = tile_tokens(j)
                        col = ((j - 1) % (TILES + 1)) * P
                        mm = pe.matmul(pv[:, 0:256], pt[0:z - a, col:col + P],
                                       v_nat[0:z - a, j, :, :].rearrange("p h d -> p (h d)"),
                                       start=(m == 0 and j == 0), stop=(m == 1 and j == TILES))
                mm.then_inc(pv_done, 1)

            def attend(n, hp, ahead):
                u = n * PAIRS + hp

                def part(k):
                    if ahead:
                        b = k // 4
                        project_half(n, PAIRS + 2 + 2 * hp + b, b, n * BUFS + PAIRS // 2 + 1 + hp, (k // 2) % 2, (k % 2,))

                at_v = n * SLICES + PAIRS + 2 * hp
                at_k = at_v + 1
                turn_v(u, 0, at_v)
                scores(u, 0, at_k)
                part(0)
                turn_v(u, 1, at_v)
                turn_p(u, 0)
                scores(u, 1, at_k)
                part(1)
                turn_v(u, 2, at_v)
                weigh(u, 0)
                turn_p(u, 1)
                scores(u, 2, at_k)
                part(2)
                turn_gq(u)
                weigh(u, 1)
                turn_p(u, 2)
                scores(u, 3, at_k)
                part(3)
                weigh(u, 2)
                turn_p(u, 3)
                global_scores(u)
                part(4)
                weigh(u, 3)
                part(5)
                turn_gp(u)
                part(6)
                global_weigh(u)
                part(7)

            with pe.Fori(0, BATCH) as n:
                for t in range(TILES):
                    pe.wait_ge(xn_set, n * TILES + t + 1)
                    if t > 0:
                        pe.wait_ge(xT_set, n * TILES + t)
                    for k in range(KC):
                        mm = pe.transpose(turn[:, k * P:k * P + P], x_norm[:, t % 2, k * P:k * P + P], ident[:, :])
                    mm.then_inc(ln_turned, 1)
                pe.wait_ge(xT_set, n * TILES + TILES)
                apart(pe)
                with pe.Fori(0, PAIRS // 2) as j:
                    for b in range(2):
                        hp = 2 * j + b
                        project_half(n, hp, b, n * BUFS + j, 0)
                        if b == 1:
                            turn_q(n, hp - 1, 1)
                        project_half(n, hp, b, n * BUFS + j, 1)
                        turn_q(n, hp, 0)
                    turn_q(n, hp, 1)
                pe.wait_ge(norm_set, n * (2 * PAIRS) + 2 * PAIRS)
                for t in range(TILES):
                    mm = pe.transpose(turn[0:HEADS, t * P:t * P + P], norms[:, t, :], ident[:, :])
                mm.then_inc(norm_turned, 1)
                for b in range(2):
                    for half in range(2):
                        project_half(n, PAIRS + b, b, n * BUFS + PAIRS // 2, half)
                with pe.Fori(0, PAIRS - 1) as hp:
                    attend(n, hp, True)
                attend(n, PAIRS - 1, False)

            for t in range(TILES):
                g = BATCH * TILES + t
                pe.wait_ge(xn_set, g + 1)
                if t > 0:
                    pe.wait_ge(xT_set, g)
                for k in range(KC):
                    mm = pe.transpose(turn[:, k * P:k * P + P], x_norm[:, t % 2, k * P:k * P + P], ident[:, :])
                mm.then_inc(ln_turned, 1)
            LIN = (BATCH + 1) * TILES

            def turn_lin(t, b):
                pe.wait_ge(xn_set, LIN + t + 1)
                pe.wait_ge(xT_set, LIN + t)
                for k in range(KC):
                    mm = pe.transpose(turn[:, k * P:k * P + P], x_norm[:, b, k * P:k * P + P], ident[:, :])
                mm.then_inc(ln_turned, 1)

            def linear(t, b, half):
                if half == 0:
                    pe.wait_ge(xT_set, LIN + t + 1)
                pe.wait_ge(o_set, 2 * t + half + 1)
                terms = [(x, w, k) for x, w in ((xlT_hi, xT_hi), (xlT_lo, xT_hi), (xlT_hi, xT_lo)) for k in range(KC)]
                for m, (x, w, k) in enumerate(terms):
                    mm = pe.matmul(proj[:, half, :], x[b][:, k * P:k * P + P], w[:, k, half * 512:half * 512 + 512],
                                   start=(m == 0), stop=(m == 23), skip_group_check=True)
                mm.then_inc(lin_done[half], 1)

            turn_lin(0, 0)
            with pe.Fori(0, OUT_TILES // 2 - 1) as j:
                for b in range(2):
                    linear(2 * j + b, b, 0)
                    turn_lin(2 * j + b + 1, 1 - b)
                    linear(2 * j + b, b, 1)
            linear(OUT_TILES - 2, 0, 0)
            turn_lin(OUT_TILES - 1, 1)
            linear(OUT_TILES - 2, 0, 1)
            linear(OUT_TILES - 1, 1, 0)
            linear(OUT_TILES - 1, 1, 1)

        @block.scalar
        def _(act):
            for h in range(2):
                act.sem_inc(proj_free[h], 1)
            act.wait_ge(const_in, 80)

            def std(g):
                act.wait_ge(ln_var_set, g + 1)
                act.activation(ln_std[:, :], ln_var[:, :], ACT.Sqrt).then_inc(ln_std_set, 1)

            turn8 = turn[:, :].rearrange("p (k t) -> p k t", k=KC)

            def tile_hi(g, dst):
                act.wait_ge(ln_turned, g + 1)
                act.copy(dst, turn8).then_inc(xT_hi_set, 1)

            def q_out(n, hp, h):
                act.wait_ge(proj_done[h], n * SLICES + hp + 1)
                apart(act)
                tok = slice(h * HALF, h * HALF + HALF)
                act.activation(qT_cur[:, tok], proj[:, h, :], ACT.Identity,
                               bias=bq_c[:, bass.ds(hp, 1)]).then_inc(qT_set[h], 1)
                act.activation(q_store[:, bass.ds(hp, 1), tok].rearrange("p a t -> p (a t)"), proj[:, h, :], ACT.Identity,
                               bias=bq_c[:, bass.ds(hp, 1)]).then_inc(proj_free[h], 1)

            def q_nat_out(n, hp, h):
                act.wait_ge(q_turned[h], n * PAIRS + hp + 1)
                act.wait_ge(q_squared[h], n * PAIRS + hp + 1)
                act.wait_ge(q_stored[h], n * (16 * PAIRS) + hp * 16 + 16)
                act.copy(q_nat[:, 4 * h:4 * h + 4, :].rearrange("p t d -> p (t d)"),
                         turn[:, h * 512:h * 512 + 512]).then_inc(q_nat_set[h], 1)

            def v_out(n, hp, h):
                act.wait_ge(proj_done[h], n * SLICES + PAIRS + 2 * hp + 1)
                apart(act)
                act.activation(vT[:, h * HALF:h * HALF + HALF], proj[:, h, :], ACT.Identity,
                               bias=bv_c[:, bass.ds(hp, 1)]).then_inc(proj_free[h], 1)

            def k_hi_out(n, hp, h):
                act.wait_ge(proj_done[h], n * SLICES + PAIRS + 2 * hp + 2)
                apart(act)
                act.activation(kT_hi[:, h * HALF:h * HALF + HALF], proj[:, h, :], ACT.Identity,
                               bias=bk_c[:, bass.ds(hp, 1)]).then_inc(k_hi_set[h], 1)

            def v_hi_out(u, g):
                act.wait_ge(m_turned, u * MISC + g + 1)
                for rows, j, step, count, col in V_PIECES[g]:
                    last = act.copy(v_nat[0:rows, j:j + step * (count - 1) + 1:step, :, 0:HD],
                                    misc[0:rows, col:col + count * P].rearrange("p (t h d) -> p t h d", h=2, d=HD))
                last.then_inc(m_hi_set, 1)

            def gq_hi_out(u):
                act.wait_ge(m_turned, u * MISC + MISC)
                act.copy(gq_hi[:, :], misc[:, 0:P]).then_inc(m_hi_set, 1)

            def exps(u, s):
                act.wait_ge(max_set, u * EVENTS + s + 1)
                for h in range(2):
                    for b in range(2):
                        lo, hi, col = window(2 * s + b)
                        at, g = h * 512 + b * 256 + col, 4 * s + 2 * h + b
                        last = act.activation(probs[:, at:at + hi - lo], score[:, at:at + hi - lo], ACT.Exp,
                                              bias=neg_max[:, g:g + 1], accum_out=row_sum[:, g:g + 1])
                last.then_inc(exp_set, 1)

            def global_exps(u):
                act.wait_ge(max_set, u * EVENTS + EVENTS)
                g = 4 * STEPS
                act.activation(probs[:, :], score[:, :], ACT.Exp, bias=neg_max[:, g:g + 1],
                               accum_out=row_sum[:, g:g + 1]).then_inc(exp_set, 1)

            def p_hi_out(u, s):
                act.wait_ge(p_turned, u * EVENTS + s + 1)
                for rows, a, size in turned_pieces(s):
                    last = act.copy(pT_hi[0:rows, 0:1024].rearrange("p (h c) -> p h c", h=2)[:, :, a:a + size],
                                    turn[0:rows, :].rearrange("p (h c) -> p h c", h=2)[:, :, a:a + size])
                last.then_inc(pT_hi_set, 1)

            def gp_hi_out(u):
                act.wait_ge(p_turned, u * EVENTS + EVENTS)
                act.copy(pT_hi[:, 0:896], turn[:, 0:896])
                act.copy(pT_hi[0:64, 896:1024], turn[0:64, 896:1024])
                act.copy(pT_hi[0:64, 1024:1152], misc[0:64, 0:P]).then_inc(pT_hi_set, 1)

            pv4 = pv[:, :].rearrange("p (g d) -> p g d", g=4)

            def pv_lo_out(u, s):
                act.wait_ge(pv_done, u * EVENTS + s + 1)
                act.copy(pv_lo[:, :, :], pv4[:, :, HD:P]).then_inc(pv_lo_set, 1)

            def g_lo_out(u):
                act.wait_ge(pv_done, u * EVENTS + EVENTS)
                act.copy(pv_lo[0:64, 0, :], pv4[0:64, 0, HD:P])
                act.copy(pv_lo[64:P, 0, :], pv4[64:P, 1, HD:P]).then_inc(pv_lo_set, 1)

            def attend(n, hp, ahead):
                u = n * PAIRS + hp
                v_hi_out(u, 0)
                exps(u, 0)
                v_hi_out(u, 1)
                p_hi_out(u, 0)
                exps(u, 1)
                if ahead:
                    v_out(n, hp + 1, 0)
                v_hi_out(u, 2)
                pv_lo_out(u, 0)
                p_hi_out(u, 1)
                exps(u, 2)
                gq_hi_out(u)
                pv_lo_out(u, 1)
                p_hi_out(u, 2)
                exps(u, 3)
                if ahead:
                    v_out(n, hp + 1, 1)
                pv_lo_out(u, 2)
                p_hi_out(u, 3)
                global_exps(u)
                pv_lo_out(u, 3)
                if ahead:
                    k_hi_out(n, hp + 1, 0)
                gp_hi_out(u)
                g_lo_out(u)
                if ahead:
                    k_hi_out(n, hp + 1, 1)

            with act.Fori(0, BATCH) as n:
                std(n * TILES)
                for t in range(TILES):
                    if t + 1 < TILES:
                        std(n * TILES + t + 1)
                    tile_hi(n * TILES + t, xT_hi[:, :, t * P:t * P + P])
                with act.Fori(0, PAIRS // 2) as j:
                    q_out(n, 2 * j, 0)
                    q_out(n, 2 * j, 1)
                    q_nat_out(n, 2 * j, 0)
                    q_out(n, 2 * j + 1, 0)
                    q_nat_out(n, 2 * j, 1)
                    q_out(n, 2 * j + 1, 1)
                    q_nat_out(n, 2 * j + 1, 0)
                    q_nat_out(n, 2 * j + 1, 1)
                act.wait_ge(norm_turned, n + 1)
                act.copy(norm_rows[:, 0, :], turn[0:HEADS, :]).then_inc(norm_rows_set, 1)
                v_out(n, 0, 0)
                v_out(n, 0, 1)
                k_hi_out(n, 0, 0)
                k_hi_out(n, 0, 1)
                with act.Fori(0, PAIRS - 1) as hp:
                    attend(n, hp, True)
                attend(n, PAIRS - 1, False)

            for t in range(TILES):
                tile_hi(BATCH * TILES + t, xT_hi[:, :, t * P:t * P + P])
            LIN = (BATCH + 1) * TILES

            def lin_hi(t, b):
                tile_hi(LIN + t, xlT_hi[b][:, :].rearrange("p (k t) -> p k t", k=KC))

            std(BATCH * TILES)
            std(BATCH * TILES + 1)
            lin_hi(0, 0)
            with act.Fori(0, OUT_TILES // 2 - 1) as j:
                for b in range(2):
                    lin_hi(2 * j + b + 1, 1 - b)
                    std(BATCH * TILES + 2 * j + b + 2)
            lin_hi(OUT_TILES - 1, 1)

        @block.vector
        def _(dve):
            dve.sem_inc(pv_free, 1)
            dve.sem_inc(o_set, 2)
            for h in range(2):
                dve.sem_inc(q_squared[h], 1)
            dve.memset(idx_f[:, TOPK - 2:TOPK - 1], 0.0)
            dve.memset(idx_f[:, TOPK - 1:TOPK], float(SEQ - 1))
            dve.memset(batch_base[:, :], 0.0)
            dve.wait_ge(const_in, 80)
            dve.wait_ge(pad_zero, 1)
            dve.wait_ge(base_set, 1)
            turn8 = turn[:, :].rearrange("p (k t) -> p k t", k=KC)

            def normalise(src, dst, g, links):
                def link(ins):
                    links[0] += 1
                    ins.then_inc(ln_step, 1)
                    dve.wait_ge(ln_step, g * LN_LINKS + links[0])

                for half in range(2):
                    last = dve.bn_stats(ln_stats[:, half, :], src[:, half * 512:half * 512 + 512])
                link(last)
                apart(dve)
                link(dve.bn_aggr(ln_mv[:, :], ln_stats[:, :, :].rearrange("p a b -> p (a b)")))
                dve.tensor_scalar(ln_var[:, :], ln_mv[:, 1:2], EPS, None, ALU.add).then_inc(ln_var_set, 1)
                dve.wait_ge(ln_std_set, g + 1)
                link(dve.reciprocal(ln_rec[:, :], ln_std[:, :]))
                link(dve.scalar_tensor_tensor(ln_two[:, :], ln_var[:, :], ln_rec[:, :], ln_std[:, :],
                                              ALU.mult, ALU.add))
                link(dve.reciprocal(ln_half[:, :], ln_two[:, :]))
                link(dve.tensor_scalar(ln_rstd[:, :], ln_half[:, :], 2.0, None, ALU.mult))
                assert links[0] == LN_LINKS
                dve.tensor_scalar(dst, src, ln_mv[:, 0:1], ln_rstd[:, :], ALU.subtract, ALU.mult).then_inc(xn_set, 1)

            def tile_lo(g, dst, hi):
                dve.wait_ge(xT_hi_set, g + 1)
                dve.tensor_tensor(dst, turn8, hi.bitcast(F32), ALU.subtract).then_inc(xT_set, 1)

            def norm_of(n, hp, h):
                dve.wait_ge(q_nat_set[h], n * PAIRS + hp + 1)
                src = q_nat[:, 4 * h:4 * h + 4, :].rearrange("p t d -> p (t d)")
                dve.tensor_tensor(q_sq[:, :], src, src, ALU.mult).then_inc(q_squared[h], 1)
                dve.wait_ge(q_squared[h], n * PAIRS + hp + 2)
                dve.tensor_reduce(norms[:, 4 * h:4 * h + 4, bass.ds(2 * hp, 2)],
                                  q_sq[:, :].rearrange("p (t h d) -> p t h d", h=2, d=HD),
                                  AX.X, ALU.add).then_inc(norm_set, 1)
                dve.wait_ge(norm_set, n * (2 * PAIRS) + 2 * hp + h + 1)

            def split_q(u, hp):
                src = q_store[:, bass.ds(hp, 1), :].rearrange("p a t -> p (a t)")
                dve.tensor_scalar(qT_hi[:, :], src, HD ** -0.5, None, ALU.mult).then_inc(qh_set, 1)
                dve.wait_ge(qh_set, u + 1)
                dve.scalar_tensor_tensor(qT_lo[:, :], src, HD ** -0.5, qT_hi[:, :].bitcast(F32),
                                         ALU.mult, ALU.subtract).then_inc(q_split, 1)

            def k_lo_out(n, hp, h):
                tok = slice(h * HALF, h * HALF + HALF)
                dve.wait_ge(k_hi_set[h], n * PAIRS + hp + 1)
                dve.scalar_tensor_tensor(kT_lo[:, tok], proj[:, h, :], bk_c[:, bass.ds(hp, 1)],
                                         kT_hi[:, tok].bitcast(F32), ALU.add, ALU.subtract).then_inc(proj_free[h], 1)

            def top_norms(n, between):
                count = [0]

                def link(ins):
                    count[0] += 1
                    ins.then_inc(top_step, 1)
                    dve.wait_ge(top_step, n * TOP_LINKS + count[0])

                rounds = TOPK // 8
                dve.wait_ge(norm_rows_set, n + 1)
                for r in range(rounds):
                    now, then = norm_rows[:, r % 2, :], norm_rows[:, 1 - r % 2, :]
                    apart(dve)
                    link(dve.max(top_val[:, :], now))
                    apart(dve)
                    dve.max_index(top_idx[:, 8 * r:8 * r + 8], top_val[:, :], now)
                    link(dve.match_replace(then, top_val[:, :], now, -1.0))
                    if r in between:
                        between[r]()
                top = TOPK - 2
                link(dve.tensor_copy(idx_f[:, 0:top], top_idx[:, 0:top]))
                for e in range(2):
                    dve.tensor_scalar(idx_eq[:, e, :], idx_f[:, 0:top], float(e * (SEQ - 1)), None, ALU.is_equal)
                link(dve.tensor_scalar(idx_row[:, :], idx_f[:, :], float(HEADS), row_base[:, :], ALU.mult, ALU.add))
                link(dve.tensor_reduce(idx_dup[:, :], idx_eq[:, :, :], AX.X, ALU.max))
                dve.tensor_copy(idx_out[:, 0, :], idx_row[:, :]).then_inc(idx_set, 1)
                link(dve.tensor_scalar(idx_dst[:, :], idx_row[:, :], batch_base[:, :], None, ALU.add))
                dve.tensor_copy(idx_out[:, 1, 0:top], idx_dst[:, 0:top])
                link(dve.scalar_tensor_tensor(idx_skip[:, top:TOPK], idx_dup[:, :], SKIP, idx_dst[:, top:TOPK],
                                              ALU.mult, ALU.add))
                dve.tensor_copy(idx_out[:, 1, top:TOPK], idx_skip[:, top:TOPK]).then_inc(idx_set, 1)
                link(dve.tensor_scalar(batch_base[:, :], batch_base[:, :], float(SEQ * HEADS), None, ALU.add))
                assert count[0] == TOP_LINKS

            def v_lo_out(u, g):
                dve.wait_ge(m_hi_set, u * MISC + g + 1)
                for rows, j, step, count, col in V_PIECES[g]:
                    tiles = slice(j, j + step * (count - 1) + 1, step)
                    last = dve.tensor_tensor(v_nat[0:rows, tiles, :, HD:P],
                                             misc[0:rows, col:col + count * P].rearrange("p (t h d) -> p t h d", h=2, d=HD),
                                             v_nat[0:rows, tiles, :, 0:HD].bitcast(F32), ALU.subtract)
                last.then_inc(m_set, 1)

            def gq_lo_out(u):
                dve.wait_ge(m_hi_set, u * MISC + MISC)
                dve.tensor_tensor(gq_lo[:, :], misc[:, 0:P], gq_hi[:, :].bitcast(F32), ALU.subtract).then_inc(m_set, 1)

            def maxima(u, s):
                dve.wait_ge(scored, u * EVENTS + s + 1)
                for b, a, z in groups(s):
                    if b is None:
                        last = dve.tensor_reduce(neg_max[:, 4 * s:4 * s + 4], score4[:, :, a:z], AX.X, ALU.max, negate=True)
                    else:
                        last = dve.tensor_reduce(neg_max[:, 4 * s + b:4 * s + b + 3:2], score4[:, b::2, a:z],
                                                 AX.X, ALU.max, negate=True)
                last.then_inc(max_set, 1)

            def global_maxima(u):
                dve.wait_ge(scored, u * EVENTS + EVENTS)
                dve.tensor_reduce(neg_max[:, 4 * STEPS:4 * STEPS + 1], score[:, :], AX.X, ALU.max,
                                  negate=True).then_inc(max_set, 1)

            def p_lo_out(u, s):
                dve.wait_ge(pT_hi_set, u * EVENTS + s + 1)
                for rows, a, size in turned_pieces(s):
                    last = dve.tensor_tensor(pT_lo[0:rows, 0:1024].rearrange("p (h c) -> p h c", h=2)[:, :, a:a + size],
                                             turn[0:rows, :].rearrange("p (h c) -> p h c", h=2)[:, :, a:a + size],
                                             pT_hi[0:rows, 0:1024].rearrange("p (h c) -> p h c", h=2)[:, :, a:a + size]
                                             .bitcast(F32), ALU.subtract)
                last.then_inc(pT_set, 1)

            def gp_lo_out(u):
                dve.wait_ge(pT_hi_set, u * EVENTS + EVENTS)
                for rows, a, src in ((P, slice(0, 896), turn[:, 0:896]), (64, slice(896, 1024), turn[0:64, 896:1024]),
                                     (64, slice(1024, 1152), misc[0:64, 0:P])):
                    last = dve.tensor_tensor(pT_lo[0:rows, a], src, pT_hi[0:rows, a].bitcast(F32), ALU.subtract)
                last.then_inc(pT_set, 1)

            def inverses(u, s):
                dve.wait_ge(exp_set, u * EVENTS + s + 1)
                if s < STEPS:
                    dve.wait_ge(ctx_set, u * STEPS + s + 1)
                size = 4 if s < STEPS else 1
                dve.reciprocal(row_inv[:, 4 * s:4 * s + size], row_sum[:, 4 * s:4 * s + size]).then_inc(inv_set, 1)

            pv4 = pv[:, :].rearrange("p (g d) -> p g d", g=4)

            def pv_sums(u, s):
                dve.wait_ge(pv_lo_set, u * EVENTS + s + 1)
                dve.wait_ge(ctx_set, u * STEPS + s + STEPS - 1)
                dve.tensor_tensor(pv_sum[:, s % 2], pv4[:, :, 0:HD], pv_lo[:, :, :], ALU.add).then_inc(pv_free, 1)

            def pad_q(n, u, hp):
                dve.wait_ge(sel_in, n * (16 * PAIRS) + 16 * PAIRS)
                for h in range(2):
                    r = slice(h * HD, h * HD + HD)
                    last = dve.tensor_scalar(q_pad[r, r], q_sel[r, bass.ds(hp, 1), :].rearrange("p a d -> p (a d)"),
                                             HD ** -0.5, None, ALU.mult)
                last.then_inc(pad_set, 1)

            def g_out(n, u, hp):
                dve.wait_ge(pv_lo_set, u * EVENTS + EVENTS)
                dve.tensor_tensor(g_sum[0:64, :], pv4[0:64, 0, 0:HD], pv_lo[0:64, 0, :], ALU.add)
                dve.tensor_tensor(g_sum[64:P, :], pv4[64:P, 1, 0:HD], pv_lo[64:P, 0, :], ALU.add).then_inc(pv_free, 1)
                dve.wait_ge(pv_free, u * EVENTS + EVENTS + 1)
                dve.tensor_scalar(g_ctx[:, bass.ds(hp, 1), :].rearrange("p a d -> p (a d)"), g_sum[:, :],
                                  row_inv[:, 4 * STEPS:4 * STEPS + 1], None, ALU.mult).then_inc(g_set, 1)

            def attend(n, hp, ahead):
                u = n * PAIRS + hp
                v_lo_out(u, 0)
                maxima(u, 0)
                v_lo_out(u, 1)
                p_lo_out(u, 0)
                maxima(u, 1)
                inverses(u, 0)
                v_lo_out(u, 2)
                pad_q(n, u, hp)
                pv_sums(u, 0)
                p_lo_out(u, 1)
                maxima(u, 2)
                inverses(u, 1)
                gq_lo_out(u)
                pv_sums(u, 1)
                p_lo_out(u, 2)
                maxima(u, 3)
                inverses(u, 2)
                pv_sums(u, 2)
                p_lo_out(u, 3)
                global_maxima(u)
                inverses(u, 3)
                pv_sums(u, 3)
                if ahead:
                    split_q(u + 1, hp + 1)
                    k_lo_out(n, hp + 1, 0)
                gp_lo_out(u)
                inverses(u, STEPS)
                g_out(n, u, hp)
                if ahead:
                    k_lo_out(n, hp + 1, 1)

            with dve.Fori(0, BATCH) as n:
                for t in range(TILES):
                    g = n * TILES + t
                    dve.wait_ge(x_in_s[t % 2], n * (16 * TILES // 2) + 16 * (t // 2) + 16)
                    if t >= 2:
                        dve.wait_ge(ln_turned, g - 1)
                    normalise(x_buf[:, t % 2, :], x_norm[:, t % 2, :], g, [0])
                    if t > 0:
                        tile_lo(g - 1, xT_lo[:, :, t * P - P:t * P], xT_hi[:, :, t * P - P:t * P])
                tile_lo(g, xT_lo[:, :, SEQ - P:SEQ], xT_hi[:, :, SEQ - P:SEQ])
                with dve.Fori(0, PAIRS // 2) as j:
                    for b, h in ((0, 0), (0, 1), (1, 0), (1, 1)):
                        norm_of(n, 2 * j + b, h)
                split_q(n * PAIRS, 0)
                top_norms(n, {3: lambda: k_lo_out(n, 0, 0), 5: lambda: k_lo_out(n, 0, 1)})
                apart(dve)
                with dve.Fori(0, PAIRS - 1) as hp:
                    attend(n, hp, True)
                attend(n, PAIRS - 1, False)

            for t in range(TILES):
                g = BATCH * TILES + t
                dve.wait_ge(x_in_s[t % 2], BATCH * (16 * TILES // 2) + 16 * (t // 2) + 16)
                if t >= 2:
                    dve.wait_ge(ln_turned, g - 1)
                dve.tensor_scalar(x_norm[:, t % 2, :], x_buf[:, t % 2, :], scale_c[:, t:t + 1], None,
                                  ALU.mult).then_inc(xn_set, 1)
                if t > 0:
                    tile_lo(g - 1, xT_lo[:, :, t * P - P:t * P], xT_hi[:, :, t * P - P:t * P])
            tile_lo(g, xT_lo[:, :, SEQ - P:SEQ], xT_hi[:, :, SEQ - P:SEQ])
            LIN = (BATCH + 1) * TILES

            IN_BASE = (BATCH + 1) * (16 * TILES // 2)

            def lin_norm(t, b, turn2):
                dve.wait_ge(x_in_s[b], IN_BASE + 32 * turn2 + 32)
                if not (isinstance(t, int) and t < 2):
                    dve.wait_ge(hb_set, t - 1)
                    dve.wait_ge(ln_turned, LIN + t - 1)
                dve.tensor_tensor(lin_h[:, b, :], x_buf[:, b, :], lin_c[:, b, :], ALU.add).then_inc(h_set, 1)
                dve.wait_ge(h_set, t + 1)
                normalise(lin_h[:, b, :], x_norm[:, b, :], BATCH * TILES + t, [0])

            def lin_lo(t, b):
                view = [x[b][:, :].rearrange("p (k t) -> p k t", k=KC) for x in (xlT_lo, xlT_hi)]
                tile_lo(LIN + t, *view)

            def lin_out(t, b, half, turn2):
                cols = slice(half * 512, half * 512 + 512)
                dve.wait_ge(lin_done[half], t + 1)
                if half == 0:
                    dve.wait_ge(hb_set, t + 1)
                    dve.wait_ge(o_stored[b], 16 * turn2 + 16)
                dve.tensor_tensor(lin_o[:, b, cols], proj[:, half, :], lin_hb[:, b, cols], ALU.add).then_inc(o_set, 1)

            lin_norm(0, 0, 0)
            lin_norm(1, 1, 0)
            lin_lo(0, 0)
            with dve.Fori(0, OUT_TILES // 2 - 1) as j:
                for b in range(2):
                    lin_out(2 * j + b, b, 0, j)
                    lin_lo(2 * j + b + 1, 1 - b)
                    lin_norm(2 * j + b + 2, b, j + 1)
                    lin_out(2 * j + b, b, 1, j)
            last = OUT_TILES // 2 - 1
            lin_out(OUT_TILES - 2, 0, 0, last)
            lin_lo(OUT_TILES - 1, 1)
            lin_out(OUT_TILES - 2, 0, 1, last)
            lin_out(OUT_TILES - 1, 1, 0, last)
            lin_out(OUT_TILES - 1, 1, 1, last)


def kernel(**inputs):
    import numpy as np
    import concourse.bacc as bacc
    from concourse.bass_utils import run_bass_kernel_spmd

    nc = bacc.Bacc("TRN2", target_bir_lowering=False, num_devices=1)

    def slices(w):
        return np.asarray(w).reshape(KC, P, PAIRS, P).transpose(2, 1, 0, 3).reshape(PAIRS, P, KC * P)

    def columns(v):
        return np.ascontiguousarray(np.asarray(v).reshape(-1, P).T)

    q, k, v = (slices(inputs[f"L0_attn_W{c}"]) for c in "qkv")
    vk = np.stack([v, k], axis=1).reshape(2 * PAIRS, P, KC * P)
    arrays = {
        "x": np.asarray(inputs["L0_attn_hidden_states"]),
        "wstream": np.concatenate([q, vk], axis=0),
        "bq": columns(inputs["L0_attn_bq"]), "bk": columns(inputs["L0_attn_bk"]), "bv": columns(inputs["L0_attn_bv"]),
        "w_ffn": np.asarray(inputs["L0_ffn_weight"]),
        "scale_ffn": columns(inputs["L0_ffn_scale_weight"]),
        "bias_ffn": np.asarray(inputs["L0_ffn_bias"]),
    }
    given, args = {}, []
    for name, a in arrays.items():
        given[f"in_{name}"] = a = np.ascontiguousarray(a)
        args.append(nc.dram_tensor(f"in_{name}", a.shape, mybir.dt.from_np(a.dtype), kind="ExternalInput").ap())
    out = nc.dram_tensor("out", (BATCH, SEQ, HID), F32, kind="ExternalOutput").ap()
    build(nc, *args, out)
    return run_bass_kernel_spmd(nc, [given], core_ids=[0]).results[0]["out"]
```

```python
from contextlib import ExitStack

import concourse.bass as bass
from concourse import mybir

F32 = mybir.dt.float32
F32R = mybir.dt.float32r
U32 = mybir.dt.uint32
ALU = mybir.AluOpType
ACT = mybir.ActivationFunctionType
AX = mybir.AxisListType

P = 128
BATCH, SEQ, HID, HEADS = 4, 1024, 1024, 16
HD = HID // HEADS
PAIRS = HEADS // 2
KC = HID // P
TILES = SEQ // P
HALF = 512
BLK = 128
STEPS = SEQ // (2 * BLK)
TOPK = 64
EPS = 1e-5
SLICES = 3 * PAIRS
BUFS = SLICES // 2
EVENTS = STEPS + 1
MISC = 4
ROUNDS = BATCH + 1
NEWTON = 3
ROOT_GUESS = 0x5F3759DF
LN_LINKS = 5 + 3 * NEWTON
SKIP = float(1 << 20)
ROWS = BATCH * SEQ * HEADS
OUT_TILES = BATCH * SEQ // P
TOP_STEPS = 3 * (TOPK // 8)
TOP_LINKS = TOP_STEPS + 5
HALF_HEADS = HEADS // 2
HALF_PAIRS = PAIRS // 2


def build(nc, rows_in, wstream, bq, bk, bv, scale_ffn, bias_ffn, out):
    q_rows = nc.dram_tensor("q_rows", (SEQ * HEADS, HD), F32, kind="Internal").ap()
    ctx_rows = nc.dram_tensor("ctx_rows", (ROWS, HD), F32, kind="Internal").ap()
    idx_dram = nc.dram_tensor("idx_dram", (BATCH, 2 * HEADS * TOPK), U32, kind="Internal").ap()
    q_tiles = q_rows.rearrange("(t p h) d -> p t (h d)", p=P, h=HEADS)
    ctx_tiles = ctx_rows.rearrange("(t p h) d -> p t (h d)", p=P, h=HEADS)
    out_tiles = out.rearrange("n (t p) c -> (n t) p c", p=P)

    with ExitStack() as ctx:
        def sb(name, shape, dt=F32):
            return ctx.enter_context(nc.sbuf_tensor(name, shape, dt))

        def sem(name):
            return ctx.enter_context(nc.semaphore(name))

        xT_hi, xT_lo = sb("xT_hi", [P, KC, SEQ], F32R), sb("xT_lo", [P, KC, SEQ], F32R)
        q_store = sb("q_store", [P, PAIRS, SEQ])
        w_raw = [sb(f"w_raw{b}", [P, KC * P]) for b in range(2)]
        w_hi = [sb(f"w_hi{b}", [P, KC * P], F32R) for b in range(2)]
        w_lo = [sb(f"w_lo{b}", [P, KC * P], F32R) for b in range(2)]
        qT_cur = sb("qT_cur", [P, SEQ])
        q_nat = sb("q_nat", [P, TILES, P])
        q_sq = sb("q_sq", [P, SEQ // 2])
        qT_hi, qT_lo = sb("qT_hi", [P, SEQ], F32R), sb("qT_lo", [P, SEQ], F32R)
        kT_hi, kT_lo = sb("kT_hi", [P, SEQ], F32R), sb("kT_lo", [P, SEQ], F32R)
        vT = sb("vT", [P, SEQ])
        v_nat = sb("v_nat", [P, TILES + 1, 2, P], F32R)
        probs = sb("probs", [P, SEQ])
        pT_hi, pT_lo = sb("pT_hi", [P, SEQ + P], F32R), sb("pT_lo", [P, SEQ + P], F32R)
        x_buf, x_norm = sb("x_buf", [P, 2, HID]), sb("x_norm", [P, 2, HID])
        ident = sb("ident", [P, P])
        bq_c, bk_c, bv_c = sb("bq_c", [P, PAIRS]), sb("bk_c", [P, PAIRS]), sb("bv_c", [P, PAIRS])
        scale_c = sb("scale_c", [P, KC])
        bias_b = sb("bias_b", [P, HID])
        ln_stats, ln_mv = sb("ln_stats", [P, TILES, 2, 6]), sb("ln_mv", [P, TILES, 2])
        ln_var, ln_bits = sb("ln_var", [P, TILES]), sb("ln_bits", [P, TILES], U32)
        ln_rstd, ln_sq, ln_less = (sb(name, [P, TILES]) for name in ("ln_rstd", "ln_sq", "ln_less"))
        ln_minus_half = sb("ln_minus_half", [P, TILES])
        ln_scale = sb("ln_scale", [P, 1])
        is_weight, zero_c = sb("is_weight", [P, 1], U32), sb("zero_c", [P, 1])
        norms = sb("norms", [P, TILES, HEADS])
        norm_rows = x_norm[0:HALF_HEADS, :, :]
        last_rows = x_buf[:, 0, :]
        top_val = sb("top_val", [HALF_HEADS, 8])
        top_idx = sb("top_idx", [HALF_HEADS, TOPK], U32)
        idx_f = sb("idx_f", [HALF_HEADS, TOPK])
        idx_eq, idx_dup = sb("idx_eq", [HALF_HEADS, 2, TOPK - 2]), sb("idx_dup", [HALF_HEADS, 2])
        idx_row, idx_dst, idx_skip = (sb(name, [HALF_HEADS, TOPK]) for name in ("idx_row", "idx_dst", "idx_skip"))
        idx_out = sb("idx_out", [HALF_HEADS, 2, TOPK], U32)
        row_base, batch_base = sb("row_base", [HALF_HEADS, 2]), sb("batch_base", [P, 1])
        idx_cols = sb("idx_cols", [P, 2, PAIRS], U32)
        q_sel = sb("q_sel", [P, PAIRS, HD])
        q_pad = sb("q_pad", [P, P])
        gq_hi, gq_lo = sb("gq_hi", [P, P], F32R), sb("gq_lo", [P, P], F32R)
        neg_max = sb("neg_max", [P, 4 * EVENTS])
        row_sum, row_inv = sb("row_sum", [P, 4 * EVENTS]), sb("row_inv", [P, 4 * EVENTS])
        pv_lo = sb("pv_lo", [P, 4, HD])
        pv_sum = sb("pv_sum", [P, 2, 4, HD])
        ctx_out = sb("ctx_out", [P, 2, 2, 2, HD])
        g_sum = sb("g_sum", [P, HD])
        g_ctx = sb("g_ctx", [P, PAIRS, HD])
        lin_c, lin_h = q_store[:, 0:2, :], q_store[:, 2:4, :]
        lin_hb, lin_o = q_store[:, 4:6, :], q_store[:, 6:8, :]
        xlT_hi, xlT_lo = [kT_hi, qT_hi], [kT_lo, qT_lo]

        proj = ctx.enter_context(nc.psum_tensor("proj", [P, 2, 512], F32))
        score = ctx.enter_context(nc.psum_tensor("score", [P, 1024], F32))
        turn = ctx.enter_context(nc.psum_tensor("turn", [P, 1024], F32))
        pv = ctx.enter_context(nc.psum_tensor("pv", [P, 512], F32))
        misc = ctx.enter_context(nc.psum_tensor("misc", [P, 512], F32))
        score4 = score[:, :].rearrange("p (g k) -> p g k", g=4)

        const_in = sem("const_in"); bias_in = sem("bias_in"); ident_zero = sem("ident_zero"); ident_set = sem("ident_set")
        base_set = sem("base_set"); pad_zero = sem("pad_zero")
        raw_in = [sem(f"raw_in{b}") for b in range(2)]
        w_hi_set = sem("w_hi_set")
        w_split = [sem(f"w_split{b}") for b in range(2)]
        first_in = [sem(f"first_in{b}") for b in range(4)]
        rows_loaded = sem("rows_loaded")
        weight_set = sem("weight_set")
        ln_step = sem("ln_step"); xn_set = sem("xn_set")
        x_turned = [sem(f"x_turned{h}") for h in range(2)]
        xT_hi_set = [sem(f"xT_hi_set{h}") for h in range(2)]
        xT_set = [sem(f"xT_set{h}") for h in range(2)]
        lin_in = [sem(f"lin_in{b}") for b in range(2)]
        ln_set = sem("ln_set"); lin_turned = sem("lin_turned"); lin_hi_set = sem("lin_hi_set"); lin_set = sem("lin_set")
        proj_done = [sem(f"proj_done{h}") for h in range(2)]
        proj_free = [sem(f"proj_free{h}") for h in range(2)]
        qT_set = [sem(f"qT_set{h}") for h in range(2)]
        q_turned = [sem(f"q_turned{h}") for h in range(2)]
        q_nat_set = [sem(f"q_nat_set{h}") for h in range(2)]
        q_squared = [sem(f"q_squared{h}") for h in range(2)]
        q_stored = [sem(f"q_stored{h}") for h in range(2)]
        norm_set = sem("norm_set"); norm_turned = sem("norm_turned"); norm_rows_set = sem("norm_rows_set")
        top_step = sem("top_step"); idx_set = sem("idx_set"); idx_dma = sem("idx_dma"); idx_cols_in = sem("idx_cols_in")
        sel_in = [sem(f"sel_in{half}") for half in range(2)]
        qh_set = sem("qh_set"); q_split = sem("q_split")
        k_hi_set = [sem(f"k_hi_set{h}") for h in range(2)]
        scored = sem("scored"); max_set = sem("max_set"); exp_set = sem("exp_set")
        p_turned = sem("p_turned"); pT_hi_set = sem("pT_hi_set"); pT_set = sem("pT_set")
        m_turned = sem("m_turned"); m_hi_set = sem("m_hi_set"); m_set = sem("m_set")
        pad_set = sem("pad_set")
        pv_done = sem("pv_done"); pv_lo_set = sem("pv_lo_set")
        pv_free = sem("pv_free")
        inv_set = sem("inv_set")
        ctx_set = sem("ctx_set")
        ctx_stored = [sem(f"ctx_stored{b}") for b in range(2)]
        g_set = sem("g_set"); scattered = sem("scattered")
        h_set = sem("h_set"); hb_set = sem("hb_set"); lin_done = [sem(f"lin_done{h}") for h in range(2)]
        o_set = sem("o_set")
        o_stored = [sem(f"o_stored{b}") for b in range(2)]

        def window(i):
            lo, hi = max(0, i * BLK - BLK // 2), min(SEQ, (i + 1) * BLK + BLK // 2)
            return lo, hi, lo - (i * BLK - BLK // 2)

        def groups(s):
            if s == 0:
                return [(0, 64, 256), (1, 0, 256)]
            if s == STEPS - 1:
                return [(0, 0, 256), (1, 0, 192)]
            return [(None, 0, 256)]

        def turned_pieces(s):
            if s == 0:
                return [(64, 0, 128), (P, 128, 384)]
            if s == STEPS - 1:
                return [(P, 0, 384), (64, 384, 128)]
            return [(P, 0, 512)]

        def tile_tokens(j):
            return max(0, P * j - 64), min(SEQ, P * j + 64)

        V_GROUPS = [[(0, 0), (8, 128), (1, 256), (2, 384)], [(3, 0), (4, 128), (5, 256), (6, 384)], [(7, 0)]]
        V_PIECES = [[(64, 0, TILES, 2, 0), (P, 1, 1, 2, 256)], [(P, 3, 1, 4, 0)], [(P, 7, 1, 1, 0)]]

        ROW_ORDER = [TILES - 1] + list(range(TILES - 1))
        LAST_TILES = [[0], [1], [2], [3], [4], [5], [6], [7]]
        proj_banks, turn_banks = [proj[:, h, :] for h in range(2)], [turn[:, h * 512:h * 512 + 512] for h in range(2)]

        passed = sem("passed")

        def apart(eng):
            eng.sem_inc(passed, 1)

        block = ctx.enter_context(nc.Block())

        @block.sync
        def _(sp):
            for b in range(2):
                sp.sem_inc(q_stored[b], 16)
                sp.sem_inc(o_stored[b], 16)
            for t in range(TILES):
                if t >= 4:
                    sp.wait_ge(first_in[t % 4], 16)
                sp.dma_start(q_store[:, t, :], rows_in[t]).then_inc(first_in[t % 4], 16)
                if t == 1:
                    for dst, src in ((bq_c, bq), (bk_c, bk), (bv_c, bv), (scale_c, scale_ffn)):
                        sp.dma_start(dst[:, :], src).then_inc(const_in, 16)

            def load_slice(n, i, b, count):
                sp.wait_ge(w_split[b], count + 1)
                sp.dma_start(w_raw[b][:, :], wstream[i]).then_inc(raw_in[b], 16)

            def store_ctx(n, hp, s):
                sp.wait_ge(ctx_set, n * (PAIRS * STEPS) + hp * STEPS + s + 1 + STEPS)
                sp.dma_start(ctx_tiles[:, bass.ds(n * TILES + 2 * s, 2), bass.ds(hp * P, P)],
                             ctx_out[:, s % 2].rearrange("p b h d -> p b (h d)")).then_inc(ctx_stored[s % 2], 16)

            def load_rows(n, hp):
                sp.wait_ge(q_split, n * PAIRS + hp + 1)
                apart(sp)
                sp.wait_ge(rows_loaded, n * (16 * TILES) + 16 * hp + 16)
                apart(sp)
                sp.dma_start(q_store[:, bass.ds(hp, 1), :].rearrange("p a c -> p (a c)"),
                             rows_in[n * TILES + hp + TILES]).then_inc(rows_loaded, 16)

            for b in range(2):
                load_slice(0, b, b, 0)
            sp.dma_start(bias_b[:, :], bias_ffn.partition_broadcast(P)).then_inc(bias_in, 16)
            with sp.Fori(0, BATCH) as n:
                for h in range(2):
                    sp.wait_ge(x_turned[h], n * TILES + 1)
                apart(sp)
                sp.wait_ge(rows_loaded, n * (16 * TILES))
                apart(sp)
                sp.dma_start(last_rows, rows_in[n * TILES + 2 * TILES - 1]).then_inc(rows_loaded, 16)
                with sp.Fori(0, PAIRS // 2) as j:
                    for b, h in ((0, 0), (0, 1), (1, 0), (1, 1)):
                        if h == 0:
                            load_slice(n, 2 * j + b + 2, b, n * BUFS + j + 1)
                        sp.wait_ge(q_nat_set[h], n * PAIRS + 2 * j + b + 1)
                        sp.dma_start(q_tiles[:, 4 * h:4 * h + 4, bass.ds((2 * j + b) * P, P)],
                                     q_nat[:, 4 * h:4 * h + 4, :]).then_inc(q_stored[h], 16)
                for b in range(2):
                    load_slice(n, PAIRS + 2 + b, b, n * BUFS + PAIRS // 2 + 1)
                with sp.Fori(0, PAIRS - 2) as hp:
                    load_rows(n, hp)
                    load_slice(n, PAIRS + 4 + 2 * hp, 0, n * BUFS + PAIRS // 2 + 2 + hp)
                    store_ctx(n, hp, 0)
                    store_ctx(n, hp, 1)
                    load_slice(n, PAIRS + 5 + 2 * hp, 1, n * BUFS + PAIRS // 2 + 2 + hp)
                    store_ctx(n, hp, 2)
                    store_ctx(n, hp, 3)
                for hp in (PAIRS - 2, PAIRS - 1):
                    if hp == PAIRS - 2:
                        load_rows(n, hp)
                        load_slice(n, 0, 0, (n + 1) * BUFS)
                    store_ctx(n, hp, 0)
                    store_ctx(n, hp, 1)
                    if hp == PAIRS - 2:
                        load_slice(n, 1, 1, (n + 1) * BUFS)
                    store_ctx(n, hp, 2)
                    store_ctx(n, hp, 3)

            def load_x(t, b):
                sp.dma_start(x_buf[:, b, :], rows_in[t]).then_inc(lin_in[b], 16)
                sp.dma_start(lin_c[:, b, :], ctx_tiles[:, t, :]).then_inc(lin_in[b], 16)

            def load_pair(j):
                for b in range(2):
                    sp.wait_ge(h_set, 2 * j + b + 1)
                    apart(sp)
                    load_x(2 * j + 2 + b, b)

            EARLY = (BATCH - 1) * TILES
            sp.wait_ge(scattered, 16 * (BATCH - 1) * PAIRS)
            for h in range(2):
                sp.wait_ge(x_turned[h], BATCH * TILES + 3)
            load_x(0, 0)
            load_x(1, 1)
            with sp.Fori(0, EARLY // 2 - 1) as j:
                load_pair(j)
            sp.wait_ge(scattered, 16 * BATCH * PAIRS)
            with sp.Fori(EARLY // 2 - 1, OUT_TILES // 2 - 1) as j:
                load_pair(j)
            for b in range(2):
                sp.wait_ge(o_stored[b], 16 + 16 * OUT_TILES // 2)

        @block.gpsimd
        def _(pool):
            for b in range(2):
                pool.sem_inc(w_split[b], 1)
                pool.sem_inc(ctx_stored[b], 16)
            pool.sem_inc(ctx_set, STEPS)
            pool.memset(ident[:, :], 0.0).then_inc(ident_zero, 1)
            pool.wait_ge(ident_zero, 1)
            pool.affine_select(out=ident[:, :], in_=ident[:, :], compare_op=ALU.not_equal, fill=1.0, base=0,
                               pattern=[[-1, P]], channel_multiplier=1).then_inc(ident_set, 1)
            pool.iota(row_base[:, :], [[HALF_HEADS, 2]], base=0, channel_multiplier=1,
                      allow_small_or_imprecise_dtypes=True).then_inc(base_set, 1)
            pool.memset(q_pad[:, :], 0.0).then_inc(pad_zero, 1)

            def split(n, i, b, count):
                pool.wait_ge(raw_in[b], 16 * count + 16)
                if not (isinstance(n, int) and i < 2):
                    pool.wait_ge(proj_done[1], n * SLICES + i - 1)
                apart(pool)
                pool.tensor_copy(w_hi[b][:, :], w_raw[b][:, :]).then_inc(w_hi_set, 1)
                pool.wait_ge(w_hi_set, n * SLICES + i + 1)
                pool.tensor_tensor(w_lo[b][:, :], w_raw[b][:, :], w_hi[b][:, :].bitcast(F32),
                                   ALU.subtract).then_inc(w_split[b], 1)

            def normalise(n, hp, s):
                u = n * PAIRS + hp
                pool.wait_ge(inv_set, u * EVENTS + s + 1)
                pool.wait_ge(pv_free, u * EVENTS + s + 2)
                pool.wait_ge(ctx_stored[s % 2], u * (16 * STEPS // 2) + 16 * (s // 2) + 16)
                pool.tensor_tensor(ctx_out[:, s % 2].rearrange("p b h d -> p h b d"),
                                   pv_sum[:, s % 2].rearrange("p (h b) d -> p h b d", h=2),
                                   row_inv[:, 4 * s:4 * s + 4].rearrange("p (h b) -> p h b", h=2).unsqueeze(3)
                                   .broadcast_to([P, 2, 2, HD]),
                                   ALU.mult).then_inc(ctx_set, 1)

            def store_rows(n, half):
                pool.wait_ge(idx_set, n * 4 + 2 * half + 2)
                apart(pool)
                rows = idx_dram[n].rearrange("(g h s) -> h g s", g=2, s=TOPK)
                pool.dma_start(rows[half * HALF_HEADS:(half + 1) * HALF_HEADS], idx_out[:, :, :]).then_inc(idx_dma, 16)

            def load_columns(n, half):
                pool.wait_ge(idx_dma, n * 32 + 16 * half + 16)
                apart(pool)
                rows = idx_dram[n].rearrange("(g e r s) -> r s g e", g=2, r=2, s=TOPK)
                pairs = slice(half * HALF_PAIRS, (half + 1) * HALF_PAIRS)
                for g in range(2):
                    for r in range(2):
                        pool.dma_start(idx_cols[r * TOPK:r * TOPK + TOPK, g, pairs], rows[r, :, g, pairs],
                                       allow_slow_non_contiguous=True).then_inc(idx_cols_in, 16)

            def gather(n, half):
                pool.wait_ge(idx_cols_in, n * 128 + 64 * half + 64)
                if half == 0:
                    for h in range(2):
                        pool.wait_ge(q_stored[h], n * (16 * PAIRS) + 16 * PAIRS + 16)
                apart(pool)
                for hp in range(half * HALF_PAIRS, (half + 1) * HALF_PAIRS):
                    pool.indirect_dma_start(q_sel[:, hp, :], None, q_rows,
                                            bass.IndirectOffsetOnAxis(ap=idx_cols[:, 0, hp:hp + 1], axis=0)
                                            ).then_inc(sel_in[half], 16)

            def unit(n, hp, second_half=False):
                split(n, PAIRS + 3 + 2 * hp, 1, n * BUFS + PAIRS // 2 + 1 + hp)
                normalise(n, hp, 0)
                normalise(n, hp, 1)
                split(n, PAIRS + 4 + 2 * hp, 0, n * BUFS + PAIRS // 2 + 2 + hp)
                normalise(n, hp, 2)
                normalise(n, hp, 3)
                if second_half:
                    store_rows(n, 1)
                    load_columns(n, 1)
                    gather(n, 1)

            for b in range(2):
                split(0, b, b, 0)
            with pool.Fori(0, BATCH) as n:
                with pool.Fori(0, PAIRS // 2) as j:
                    for b in range(2):
                        split(n, 2 * j + b + 2, b, n * BUFS + j + 1)
                store_rows(n, 0)
                split(n, PAIRS + 2, 0, n * BUFS + PAIRS // 2 + 1)
                load_columns(n, 0)
                gather(n, 0)
                apart(pool)
                with pool.Fori(0, HALF_PAIRS - 1) as hp:
                    unit(n, hp)
                unit(n, HALF_PAIRS - 1, second_half=True)
                apart(pool)
                with pool.Fori(HALF_PAIRS, PAIRS - 2) as hp:
                    unit(n, hp)
                split(n, SLICES - 1, 1, n * BUFS + BUFS - 1)
                for s in range(STEPS):
                    normalise(n, PAIRS - 2, s)
                for b in range(2):
                    split(n + 1, b, b, (n + 1) * BUFS)
                    normalise(n, PAIRS - 1, 2 * b)
                    normalise(n, PAIRS - 1, 2 * b + 1)
                for b in range(2):
                    pool.wait_ge(ctx_stored[b], (n + 1) * (16 * PAIRS * STEPS // 2) + 16)
                pool.wait_ge(g_set, n * PAIRS + PAIRS)
                apart(pool)
                for hp in range(PAIRS):
                    pool.indirect_dma_start(ctx_rows, bass.IndirectOffsetOnAxis(ap=idx_cols[:, 1, hp:hp + 1], axis=0),
                                            g_ctx[:, hp, :], None, bounds_check=ROWS - 1, oob_is_err=False
                                            ).then_inc(scattered, 16)
                pool.wait_ge(scattered, (n + 1) * (16 * PAIRS))

            pool.wait_ge(bias_in, 16)

            def add_bias(t, b):
                pool.wait_ge(h_set, t + 1)
                pool.tensor_tensor(lin_hb[:, b, :], lin_h[:, b, :], bias_b[:, :], ALU.add).then_inc(hb_set, 1)

            add_bias(0, 0)
            add_bias(1, 1)
            with pool.Fori(1, OUT_TILES // 2) as j:
                for b in range(2):
                    pool.wait_ge(o_set, 4 * j + 2 * b)
                    add_bias(2 * j + b, b)

        @block.tensor
        def _(pe):
            pe.wait_ge(ident_set, 1)

            def project(b, half, part):
                terms = [(w, x, k) for w, x in ((w_hi, xT_hi), (w_lo, xT_hi), (w_hi, xT_lo)) for k in range(KC)]
                for m in range(12 * part, 12 * part + 12):
                    w, x, k = terms[m]
                    mm = pe.matmul(proj[:, half, :], w[b][:, k * P:k * P + P], x[:, k, half * HALF:half * HALF + HALF],
                                   start=(m == 0), stop=(m == 23), skip_group_check=True)
                return mm

            def project_half(n, i, b, count, half, parts=(0, 1)):
                for part in parts:
                    if part == 0:
                        if half == 0:
                            pe.wait_ge(w_split[b], count + 2)
                        pe.wait_ge(proj_free[half], n * SLICES + i + 1)
                    mm = project(b, half, part)
                    if part == 1:
                        mm.then_inc(proj_done[half], 1)

            def turn_rows(src, g, bank, banks=1):
                for h in range(2):
                    pe.wait_ge(xn_set, g + 1)
                    if not (isinstance(g, int) and g < banks):
                        pe.wait_ge(xT_set[h], g + 1 - banks)
                    apart(pe)
                    for k in range(KC // 2):
                        c = h * HALF + k * P
                        mm = pe.transpose(bank[h][:, k * P:k * P + P], src[:, c:c + P], ident[:, :])
                    mm.then_inc(x_turned[h], 1)

            def turn_q(n, hp, h):
                pe.wait_ge(qT_set[h], n * PAIRS + hp + 1)
                for t in range(4):
                    last = pe.transpose(turn[:, h * 512 + t * P:h * 512 + t * P + P],
                                        qT_cur[:, h * HALF + t * P:h * HALF + t * P + P], ident[:, :])
                last.then_inc(q_turned[h], 1)

            def turn_norms(n, half):
                pe.wait_ge(norm_set, n * (2 * PAIRS) + (half + 1) * PAIRS)
                apart(pe)
                heads = slice(half * HALF_HEADS, (half + 1) * HALF_HEADS)
                for t in range(TILES):
                    mm = pe.transpose(score[0:HALF_HEADS, t * P:t * P + P], norms[:, t, heads], ident[:, :])
                mm.then_inc(norm_turned, 1)

            def project_q(n, j, norms_too=False):
                project_half(n, 2 * j, 0, n * BUFS + j, 1)
                turn_q(n, 2 * j, 0)
                if norms_too:
                    turn_norms(n, 0)
                project_half(n, 2 * j + 1, 1, n * BUFS + j, 0)
                turn_q(n, 2 * j, 1)
                project_half(n, 2 * j + 1, 1, n * BUFS + j, 1)
                turn_q(n, 2 * j + 1, 0)
                project_half(n, 2 * j + 2, 0, n * BUFS + j + 1, 0)
                turn_q(n, 2 * j + 1, 1)

            def scores(u, s, at_k):
                if s == 0:
                    pe.wait_ge(q_split, u + 1)
                if s < 2:
                    pe.wait_ge(proj_free[s], at_k + 2)
                for qs, ks, first, stop in ((qT_hi, kT_hi, True, False), (qT_lo, kT_hi, False, False),
                                            (qT_hi, kT_lo, False, True)):
                    for b in range(2):
                        i = 2 * s + b
                        lo, hi, col = window(i)
                        for h in range(2):
                            r = slice(h * HD, h * HD + HD)
                            at = h * 512 + b * 256 + col
                            mm = pe.matmul(score[:, at:at + hi - lo], qs[r, i * BLK:i * BLK + BLK], ks[r, lo:hi],
                                           start=(first and b == 0), stop=stop, skip_group_check=True)
                mm.then_inc(scored, 1)

            def turn_p(u, s):
                pe.wait_ge(exp_set, u * EVENTS + s + 1)
                if s == 0:
                    apart(pe)
                for h in range(2):
                    for b in range(2):
                        for c in range(2):
                            a, z = tile_tokens(2 * s + b + c)
                            rows = z - a
                            col = h * 512 + b * 256 + c * P
                            src = col + (64 if (rows < P and c == 0) else 0)
                            mm = pe.transpose(turn[0:rows, col:col + P], probs[:, src:src + rows], ident[:, :])
                mm.then_inc(p_turned, 1)

            def weigh(u, s):
                pe.wait_ge(pT_set, u * EVENTS + s + 1)
                pe.wait_ge(pv_free, u * EVENTS + s + 1)
                for h in range(2):
                    for b in range(2):
                        g = h * 2 + b
                        for m, (pt, c) in enumerate(((pT_hi, 0), (pT_hi, 1), (pT_lo, 0), (pT_lo, 1))):
                            a, z = tile_tokens(2 * s + b + c)
                            rows = z - a
                            mm = pe.matmul(pv[:, g * P:g * P + P], pt[0:rows, (g * 2 + c) * P:(g * 2 + c) * P + P],
                                           v_nat[0:rows, 2 * s + b + c, h, :], start=(m == 0), stop=(m == 3))
                mm.then_inc(pv_done, 1)

            def turn_v(u, g, at_v):
                if g == 0:
                    for h in range(2):
                        pe.wait_ge(proj_free[h], at_v + 2)
                else:
                    pe.wait_ge(m_set, u * MISC + g)
                apart(pe)
                for j, col in V_GROUPS[g]:
                    a, z = tile_tokens(j)
                    mm = pe.transpose(misc[0:z - a, col:col + P], vT[:, a:z], ident[:, :])
                mm.then_inc(m_turned, 1)

            def turn_gq(u):
                pe.wait_ge(m_set, u * MISC + 3)
                pe.wait_ge(pad_set, u + 1)
                pe.transpose(misc[:, 0:P], q_pad[:, :], ident[:, :]).then_inc(m_turned, 1)

            def global_scores(u):
                pe.wait_ge(m_set, u * MISC + 4)
                for qs, ks, first, stop in ((gq_hi, kT_hi, True, False), (gq_lo, kT_hi, False, False),
                                            (gq_hi, kT_lo, False, True)):
                    for h in range(2):
                        mm = pe.matmul(score[:, h * 512:h * 512 + 512], qs[:, :], ks[:, h * 512:h * 512 + 512],
                                       start=first, stop=stop, skip_group_check=True)
                mm.then_inc(scored, 1)

            def turn_gp(u):
                pe.wait_ge(exp_set, u * EVENTS + EVENTS)
                apart(pe)
                for j in range(TILES + 1):
                    a, z = tile_tokens(j)
                    dst = turn[0:z - a, (j - 1) * P:j * P] if 0 < j else misc[0:64, 0:P]
                    mm = pe.transpose(dst, probs[:, a:z], ident[:, :])
                mm.then_inc(p_turned, 1)

            def global_weigh(u):
                pe.wait_ge(pT_set, u * EVENTS + EVENTS)
                pe.wait_ge(pv_free, u * EVENTS + EVENTS)
                for m, pt in enumerate((pT_hi, pT_lo)):
                    for j in range(TILES + 1):
                        a, z = tile_tokens(j)
                        col = ((j - 1) % (TILES + 1)) * P
                        mm = pe.matmul(pv[:, 0:256], pt[0:z - a, col:col + P],
                                       v_nat[0:z - a, j, :, :].rearrange("p h d -> p (h d)"),
                                       start=(m == 0 and j == 0), stop=(m == 1 and j == TILES))
                mm.then_inc(pv_done, 1)

            def attend(n, hp, ahead):
                u = n * PAIRS + hp

                def part(k):
                    if not ahead:
                        if k == 0:
                            pe.wait_ge(proj_free[1], at_k + 2)
                        for i in LAST_TILES[k]:
                            t = ROW_ORDER[i]
                            turn_rows(last_rows if i == 0 else q_store[:, t, :], (n + 1) * TILES + i, proj_banks)
                    else:
                        b = k // 4
                        project_half(n, PAIRS + 2 + 2 * hp + b, b, n * BUFS + PAIRS // 2 + 1 + hp, (k // 2) % 2, (k % 2,))

                at_v = n * SLICES + PAIRS + 2 * hp
                at_k = at_v + 1
                scores(u, 0, at_k)
                turn_v(u, 0, at_v)
                part(0)
                turn_v(u, 1, at_v)
                turn_p(u, 0)
                scores(u, 1, at_k)
                part(1)
                turn_v(u, 2, at_v)
                weigh(u, 0)
                turn_p(u, 1)
                scores(u, 2, at_k)
                part(2)
                weigh(u, 1)
                turn_p(u, 2)
                scores(u, 3, at_k)
                part(3)
                weigh(u, 2)
                turn_gq(u)
                turn_p(u, 3)
                part(4)
                global_scores(u)
                weigh(u, 3)
                part(5)
                turn_gp(u)
                part(6)
                part(7)
                global_weigh(u)

            for t in range(TILES):
                turn_rows(q_store[:, t, :], t, (proj_banks, turn_banks)[t % 2], 2)
            with pe.Fori(0, BATCH) as n:
                for h in range(2):
                    pe.wait_ge(xT_set[h], (n + 1) * TILES)
                apart(pe)
                project_half(n, 0, 0, n * BUFS, 0)
                with pe.Fori(0, PAIRS // 4) as j:
                    project_q(n, j)
                project_q(n, PAIRS // 4, norms_too=True)
                with pe.Fori(PAIRS // 4 + 1, PAIRS // 2) as j:
                    project_q(n, j)
                project_half(n, PAIRS, 0, n * BUFS + PAIRS // 2, 1, (0,))
                turn_norms(n, 1)
                project_half(n, PAIRS, 0, n * BUFS + PAIRS // 2, 1, (1,))
                for half in range(2):
                    project_half(n, PAIRS + 1, 1, n * BUFS + PAIRS // 2, half)
                with pe.Fori(0, PAIRS - 1) as hp:
                    attend(n, hp, True)
                attend(n, PAIRS - 1, False)

            def turn_lin(t, b):
                pe.wait_ge(ln_set, t + 1)
                if not (isinstance(t, int) and t == 0):
                    pe.wait_ge(lin_set, t)
                for k in range(KC):
                    mm = pe.transpose(turn[:, k * P:k * P + P], x_norm[:, b, k * P:k * P + P], ident[:, :])
                mm.then_inc(lin_turned, 1)

            def linear(t, b, half):
                if half == 0:
                    pe.wait_ge(lin_set, t + 1)
                pe.wait_ge(o_set, 2 * t + half + 1)
                terms = [(x, w, k) for x, w in ((xlT_hi, xT_hi), (xlT_lo, xT_hi), (xlT_hi, xT_lo)) for k in range(KC)]
                for m, (x, w, k) in enumerate(terms):
                    mm = pe.matmul(proj[:, half, :], x[b][:, k * P:k * P + P], w[:, k, half * 512:half * 512 + 512],
                                   start=(m == 0), stop=(m == 23), skip_group_check=True)
                mm.then_inc(lin_done[half], 1)

            turn_lin(0, 0)
            for h in range(2):
                pe.wait_ge(xT_set[h], ROUNDS * TILES)
            with pe.Fori(0, OUT_TILES // 2 - 1) as j:
                for b in range(2):
                    linear(2 * j + b, b, 0)
                    turn_lin(2 * j + b + 1, 1 - b)
                    linear(2 * j + b, b, 1)
            linear(OUT_TILES - 2, 0, 0)
            turn_lin(OUT_TILES - 1, 1)
            linear(OUT_TILES - 2, 0, 1)
            linear(OUT_TILES - 1, 1, 0)
            linear(OUT_TILES - 1, 1, 1)

        @block.scalar
        def _(act):
            for h in range(2):
                act.sem_inc(proj_free[h], 1)
            act.wait_ge(const_in, 64)

            turn8 = turn[:, :].rearrange("p (k t) -> p k t", k=KC)

            def rows_hi(g, t, bank):
                for h in range(2):
                    act.wait_ge(x_turned[h], g + 1)
                    act.copy(xT_hi[:, 4 * h:4 * h + 4, t * P:t * P + P],
                             bank[h].rearrange("p (k t) -> p k t", t=P)).then_inc(xT_hi_set[h], 1)

            def q_out(n, hp, h):
                act.wait_ge(proj_done[h], n * SLICES + hp + 1)
                apart(act)
                tok = slice(h * HALF, h * HALF + HALF)
                act.activation(qT_cur[:, tok], proj[:, h, :], ACT.Identity,
                               bias=bq_c[:, bass.ds(hp, 1)]).then_inc(qT_set[h], 1)
                act.activation(q_store[:, bass.ds(hp, 1), tok].rearrange("p a t -> p (a t)"), proj[:, h, :], ACT.Identity,
                               bias=bq_c[:, bass.ds(hp, 1)]).then_inc(proj_free[h], 1)

            def q_nat_out(n, hp, h):
                act.wait_ge(q_turned[h], n * PAIRS + hp + 1)
                act.wait_ge(q_squared[h], n * PAIRS + hp + 1)
                act.wait_ge(q_stored[h], n * (16 * PAIRS) + hp * 16 + 16)
                act.copy(q_nat[:, 4 * h:4 * h + 4, :].rearrange("p t d -> p (t d)"),
                         turn[:, h * 512:h * 512 + 512]).then_inc(q_nat_set[h], 1)

            def norms_out(n, half):
                act.wait_ge(norm_turned, n * 2 + half + 1)
                act.wait_ge(top_step, n * (2 * TOP_LINKS) + half * TOP_LINKS)
                apart(act)
                act.copy(norm_rows[:, 0, :], score[0:HALF_HEADS, :]).then_inc(norm_rows_set, 1)

            def q_pairs_out(n, j, norms_too=False):
                q_out(n, 2 * j, 0)
                q_out(n, 2 * j, 1)
                q_nat_out(n, 2 * j, 0)
                if norms_too:
                    norms_out(n, 0)
                q_out(n, 2 * j + 1, 0)
                q_nat_out(n, 2 * j, 1)
                q_out(n, 2 * j + 1, 1)
                q_nat_out(n, 2 * j + 1, 0)
                q_nat_out(n, 2 * j + 1, 1)

            def v_out(n, hp, h):
                act.wait_ge(proj_done[h], n * SLICES + PAIRS + 2 * hp + 1)
                apart(act)
                act.activation(vT[:, h * HALF:h * HALF + HALF], proj[:, h, :], ACT.Identity,
                               bias=bv_c[:, bass.ds(hp, 1)]).then_inc(proj_free[h], 1)

            def k_hi_out(n, hp, h):
                act.wait_ge(proj_done[h], n * SLICES + PAIRS + 2 * hp + 2)
                apart(act)
                act.activation(kT_hi[:, h * HALF:h * HALF + HALF], proj[:, h, :], ACT.Identity,
                               bias=bk_c[:, bass.ds(hp, 1)]).then_inc(k_hi_set[h], 1)

            def v_hi_out(u, g):
                act.wait_ge(m_turned, u * MISC + g + 1)
                for rows, j, step, count, col in V_PIECES[g]:
                    last = act.copy(v_nat[0:rows, j:j + step * (count - 1) + 1:step, :, 0:HD],
                                    misc[0:rows, col:col + count * P].rearrange("p (t h d) -> p t h d", h=2, d=HD))
                last.then_inc(m_hi_set, 1)

            def gq_hi_out(u):
                act.wait_ge(m_turned, u * MISC + MISC)
                act.copy(gq_hi[:, :], misc[:, 0:P]).then_inc(m_hi_set, 1)

            def exps(u, s):
                act.wait_ge(max_set, u * EVENTS + s + 1)
                for h in range(2):
                    for b in range(2):
                        lo, hi, col = window(2 * s + b)
                        at, g = h * 512 + b * 256 + col, 4 * s + 2 * h + b
                        last = act.activation(probs[:, at:at + hi - lo], score[:, at:at + hi - lo], ACT.Exp,
                                              bias=neg_max[:, g:g + 1], accum_out=row_sum[:, g:g + 1])
                last.then_inc(exp_set, 1)

            def global_exps(u):
                act.wait_ge(max_set, u * EVENTS + EVENTS)
                g = 4 * STEPS
                act.activation(probs[:, :], score[:, :], ACT.Exp, bias=neg_max[:, g:g + 1],
                               accum_out=row_sum[:, g:g + 1]).then_inc(exp_set, 1)

            def p_hi_out(u, s):
                act.wait_ge(p_turned, u * EVENTS + s + 1)
                for rows, a, size in turned_pieces(s):
                    last = act.copy(pT_hi[0:rows, 0:1024].rearrange("p (h c) -> p h c", h=2)[:, :, a:a + size],
                                    turn[0:rows, :].rearrange("p (h c) -> p h c", h=2)[:, :, a:a + size])
                last.then_inc(pT_hi_set, 1)

            def gp_hi_out(u):
                act.wait_ge(p_turned, u * EVENTS + EVENTS)
                act.copy(pT_hi[:, 0:896], turn[:, 0:896])
                act.copy(pT_hi[0:64, 896:1024], turn[0:64, 896:1024])
                act.copy(pT_hi[0:64, 1024:1152], misc[0:64, 0:P]).then_inc(pT_hi_set, 1)

            pv4 = pv[:, :].rearrange("p (g d) -> p g d", g=4)

            def pv_lo_out(u, s):
                act.wait_ge(pv_done, u * EVENTS + s + 1)
                act.copy(pv_lo[:, :, :], pv4[:, :, HD:P]).then_inc(pv_lo_set, 1)

            def g_lo_out(u):
                act.wait_ge(pv_done, u * EVENTS + EVENTS)
                act.copy(pv_lo[0:64, 0, :], pv4[0:64, 0, HD:P])
                act.copy(pv_lo[64:P, 0, :], pv4[64:P, 1, HD:P]).then_inc(pv_lo_set, 1)

            def attend(n, hp, ahead):
                u = n * PAIRS + hp

                def next_rows(k):
                    if not ahead:
                        for i in LAST_TILES[k]:
                            rows_hi((n + 1) * TILES + i, ROW_ORDER[i], proj_banks)

                v_hi_out(u, 0)
                exps(u, 0)
                next_rows(0)
                v_hi_out(u, 1)
                p_hi_out(u, 0)
                exps(u, 1)
                if ahead:
                    v_out(n, hp + 1, 0)
                next_rows(1)
                v_hi_out(u, 2)
                pv_lo_out(u, 0)
                p_hi_out(u, 1)
                exps(u, 2)
                next_rows(2)
                pv_lo_out(u, 1)
                p_hi_out(u, 2)
                exps(u, 3)
                if ahead:
                    v_out(n, hp + 1, 1)
                next_rows(3)
                pv_lo_out(u, 2)
                gq_hi_out(u)
                p_hi_out(u, 3)
                next_rows(4)
                global_exps(u)
                pv_lo_out(u, 3)
                if ahead:
                    k_hi_out(n, hp + 1, 0)
                next_rows(5)
                gp_hi_out(u)
                next_rows(6)
                if ahead:
                    k_hi_out(n, hp + 1, 1)
                next_rows(7)
                g_lo_out(u)

            for t in range(TILES):
                rows_hi(t, t, (proj_banks, turn_banks)[t % 2])
            with act.Fori(0, BATCH) as n:
                with act.Fori(0, PAIRS // 4) as j:
                    q_pairs_out(n, j)
                q_pairs_out(n, PAIRS // 4, norms_too=True)
                with act.Fori(PAIRS // 4 + 1, PAIRS // 2) as j:
                    q_pairs_out(n, j)
                v_out(n, 0, 0)
                norms_out(n, 1)
                v_out(n, 0, 1)
                k_hi_out(n, 0, 0)
                k_hi_out(n, 0, 1)
                with act.Fori(0, PAIRS - 1) as hp:
                    attend(n, hp, True)
                attend(n, PAIRS - 1, False)

            def lin_hi(t, b):
                act.wait_ge(lin_turned, t + 1)
                act.copy(xlT_hi[b][:, :].rearrange("p (k t) -> p k t", k=KC), turn8).then_inc(lin_hi_set, 1)

            def store_out(t, b):
                act.wait_ge(o_set, 2 * t + 4)
                apart(act)
                act.dma_start(out_tiles[t], lin_o[:, b, :]).then_inc(o_stored[b], 16)

            lin_hi(0, 0)
            lin_hi(1, 1)
            with act.Fori(0, OUT_TILES // 2 - 1) as j:
                for b in range(2):
                    store_out(2 * j + b, b)
                    lin_hi(2 * j + b + 2, b)
            for b in range(2):
                store_out(OUT_TILES - 2 + b, b)

        @block.vector
        def _(dve):
            dve.sem_inc(pv_free, 1)
            dve.sem_inc(o_set, 2)
            for h in range(2):
                dve.sem_inc(q_squared[h], 1)
            dve.memset(idx_f[:, TOPK - 2:TOPK - 1], 0.0)
            dve.memset(idx_f[:, TOPK - 1:TOPK], float(SEQ - 1))
            dve.memset(batch_base[:, :], 0.0)
            dve.memset(zero_c[:, :], 0.0)
            turn8 = turn[:, :].rearrange("p (k t) -> p k t", k=KC)

            def link_of(steps, links):
                def link(ins):
                    links[0] += 1
                    ins.then_inc(ln_step, 1)
                    dve.wait_ge(ln_step, steps + links[0])
                return link

            def moments(src, i, last=True):
                for half in range(2):
                    stats = dve.bn_stats(ln_stats[:, i, half, :], src[:, half * 512:half * 512 + 512])
                if last:
                    stats.then_inc(ln_step, 1)

            def roots(steps, size=1, weight_scale=None):
                links = [1]
                link = link_of(steps, links)
                var, minus_half, bits, rstd, sq, less = (x[:, 0:size] for x in (ln_var, ln_minus_half, ln_bits, ln_rstd,
                                                                                ln_sq, ln_less))
                dve.wait_ge(ln_step, steps + 1)
                apart(dve)
                for i in range(size):
                    last = dve.bn_aggr(ln_mv[:, i, :], ln_stats[:, i, :, :].rearrange("p a b -> p (a b)"))
                link(last)
                dve.tensor_scalar(minus_half, ln_mv[:, 0:size, 1], EPS, -0.5, ALU.add, ALU.mult)
                link(dve.tensor_scalar(var, ln_mv[:, 0:size, 1], EPS, None, ALU.add))
                link(dve.tensor_scalar(bits, var.bitcast(U32), 1, None, ALU.logical_shift_right))
                link(dve.tensor_scalar(rstd.bitcast(U32), bits, -1.0, float(ROOT_GUESS), ALU.mult, ALU.add))
                for _ in range(NEWTON):
                    link(dve.tensor_tensor(sq, rstd, rstd, ALU.mult))
                    link(dve.tensor_tensor(less, sq, minus_half, ALU.mult))
                    link(dve.scalar_tensor_tensor(rstd, less, 1.5, rstd, ALU.add, ALU.mult))
                assert links[0] == LN_LINKS
                if weight_scale is not None:
                    link(dve.tensor_copy(ln_scale[:, :], weight_scale))
                    apart(dve)
                    dve.copy_predicated(ln_mv[:, 0, 0:1], is_weight[:, :], zero_c[:, :])
                    link(dve.copy_predicated(ln_rstd[:, 0:1], is_weight[:, :], ln_scale[:, :]))

            def normalise(src, dst, i, done):
                dve.tensor_scalar(dst, src, ln_mv[:, i, 0:1], ln_rstd[:, i:i + 1], ALU.subtract, ALU.mult).then_inc(done, 1)

            FIRST_STEPS = LN_LINKS
            ROW_STEPS = BATCH * TILES * (LN_LINKS + 2)

            def row_moments(n, i, tile):
                g = n * TILES + i
                dve.wait_ge(rows_loaded, g * 16 + 16)
                dve.wait_ge(xn_set, g + TILES)
                moments(tile, 0)

            def row_roots(n, i, scale):
                roots((n * TILES + i) * (LN_LINKS + 2) + FIRST_STEPS, 1, scale)

            def row_normalise(tile):
                normalise(tile, tile, 0, xn_set)

            def last_tile(n):
                dve.tensor_scalar(is_weight[:, :], batch_base[:, :], float(ROWS - SEQ * HEADS), None, ALU.is_ge
                                  ).then_inc(weight_set, 1)
                dve.wait_ge(weight_set, n + 1)
                row_moments(n, 0, last_rows)
                row_roots(n, 0, scale_c[:, KC - 1:KC])
                row_normalise(last_rows)

            def rows_lo(g, t, bank):
                for h in range(2):
                    dve.wait_ge(xT_hi_set[h], g + 1)
                    at = (slice(None), slice(4 * h, 4 * h + 4), slice(t * P, t * P + P))
                    dve.tensor_tensor(xT_lo[at], bank[h].rearrange("p (k t) -> p k t", t=P), xT_hi[at].bitcast(F32),
                                      ALU.subtract).then_inc(xT_set[h], 1)

            def norm_of(n, hp, h):
                dve.wait_ge(q_nat_set[h], n * PAIRS + hp + 1)
                src = q_nat[:, 4 * h:4 * h + 4, :].rearrange("p t d -> p (t d)")
                dve.tensor_tensor(q_sq[:, :], src, src, ALU.mult).then_inc(q_squared[h], 1)
                dve.wait_ge(q_squared[h], n * PAIRS + hp + 2)
                dve.tensor_reduce(norms[:, 4 * h:4 * h + 4, bass.ds(2 * hp, 2)],
                                  q_sq[:, :].rearrange("p (t h d) -> p t h d", h=2, d=HD),
                                  AX.X, ALU.add).then_inc(norm_set, 1)
                dve.wait_ge(norm_set, n * (2 * PAIRS) + 2 * hp + h + 1)

            def split_q(u, hp):
                src = q_store[:, bass.ds(hp, 1), :].rearrange("p a t -> p (a t)")
                dve.tensor_scalar(qT_hi[:, :], src, HD ** -0.5, None, ALU.mult).then_inc(qh_set, 1)
                dve.wait_ge(qh_set, u + 1)
                dve.scalar_tensor_tensor(qT_lo[:, :], src, HD ** -0.5, qT_hi[:, :].bitcast(F32),
                                         ALU.mult, ALU.subtract).then_inc(q_split, 1)

            def k_lo_out(n, hp, h):
                tok = slice(h * HALF, h * HALF + HALF)
                dve.wait_ge(k_hi_set[h], n * PAIRS + hp + 1)
                dve.scalar_tensor_tensor(kT_lo[:, tok], proj[:, h, :], bk_c[:, bass.ds(hp, 1)],
                                         kT_hi[:, tok].bitcast(F32), ALU.add, ALU.subtract).then_inc(proj_free[h], 1)

            def top_link(n, half, k, ins):
                ins.then_inc(top_step, 1)
                dve.wait_ge(top_step, n * (2 * TOP_LINKS) + half * TOP_LINKS + k)

            def top_find(n, half, k):
                r, step = divmod(k, 3)
                now, then = norm_rows[:, r % 2, :], norm_rows[:, 1 - r % 2, :]
                if k == 0:
                    dve.wait_ge(norm_rows_set, n * 2 + half + 1)
                apart(dve)
                if step == 0:
                    ins = dve.max(top_val[:, :], now)
                elif step == 1:
                    ins = dve.max_index(top_idx[:, 8 * r:8 * r + 8], top_val[:, :], now)
                else:
                    ins = dve.match_replace(then, top_val[:, :], now, -1.0)
                top_link(n, half, k + 1, ins)

            def top_rows(n, half):
                top, k = TOPK - 2, TOP_STEPS
                base = batch_base[0:HALF_HEADS, :]
                top_link(n, half, k + 1, dve.tensor_copy(idx_f[:, 0:top], top_idx[:, 0:top]))
                for e in range(2):
                    dve.tensor_scalar(idx_eq[:, e, :], idx_f[:, 0:top], float(e * (SEQ - 1)), None, ALU.is_equal)
                top_link(n, half, k + 2, dve.tensor_scalar(idx_row[:, :], idx_f[:, :], float(HEADS),
                                                           row_base[:, half:half + 1], ALU.mult, ALU.add))
                top_link(n, half, k + 3, dve.tensor_reduce(idx_dup[:, :], idx_eq[:, :, :], AX.X, ALU.max))
                dve.wait_ge(idx_dma, n * 32 + 16 * half)
                apart(dve)
                dve.tensor_copy(idx_out[:, 0, :], idx_row[:, :]).then_inc(idx_set, 1)
                top_link(n, half, k + 4, dve.tensor_scalar(idx_dst[:, :], idx_row[:, :], base, None, ALU.add))
                dve.tensor_copy(idx_out[:, 1, 0:top], idx_dst[:, 0:top])
                top_link(n, half, k + 5, dve.scalar_tensor_tensor(idx_skip[:, top:TOPK], idx_dup[:, :], SKIP,
                                                                  idx_dst[:, top:TOPK], ALU.mult, ALU.add))
                dve.tensor_copy(idx_out[:, 1, top:TOPK], idx_skip[:, top:TOPK]).then_inc(idx_set, 1)
                if half == 1:
                    dve.tensor_scalar(batch_base[:, :], batch_base[:, :], float(SEQ * HEADS), None, ALU.add
                                      ).then_inc(base_set, 1)
                    dve.wait_ge(base_set, n + 2)

            def v_lo_out(u, g):
                dve.wait_ge(m_hi_set, u * MISC + g + 1)
                for rows, j, step, count, col in V_PIECES[g]:
                    tiles = slice(j, j + step * (count - 1) + 1, step)
                    last = dve.tensor_tensor(v_nat[0:rows, tiles, :, HD:P],
                                             misc[0:rows, col:col + count * P].rearrange("p (t h d) -> p t h d", h=2, d=HD),
                                             v_nat[0:rows, tiles, :, 0:HD].bitcast(F32), ALU.subtract)
                last.then_inc(m_set, 1)

            def gq_lo_out(u):
                dve.wait_ge(m_hi_set, u * MISC + MISC)
                dve.tensor_tensor(gq_lo[:, :], misc[:, 0:P], gq_hi[:, :].bitcast(F32), ALU.subtract).then_inc(m_set, 1)

            def maxima(u, s):
                dve.wait_ge(scored, u * EVENTS + s + 1)
                for b, a, z in groups(s):
                    if b is None:
                        last = dve.tensor_reduce(neg_max[:, 4 * s:4 * s + 4], score4[:, :, a:z], AX.X, ALU.max, negate=True)
                    else:
                        last = dve.tensor_reduce(neg_max[:, 4 * s + b:4 * s + b + 3:2], score4[:, b::2, a:z],
                                                 AX.X, ALU.max, negate=True)
                last.then_inc(max_set, 1)

            def global_maxima(u):
                dve.wait_ge(scored, u * EVENTS + EVENTS)
                dve.tensor_reduce(neg_max[:, 4 * STEPS:4 * STEPS + 1], score[:, :], AX.X, ALU.max,
                                  negate=True).then_inc(max_set, 1)

            def p_lo_out(u, s):
                dve.wait_ge(pT_hi_set, u * EVENTS + s + 1)
                for rows, a, size in turned_pieces(s):
                    last = dve.tensor_tensor(pT_lo[0:rows, 0:1024].rearrange("p (h c) -> p h c", h=2)[:, :, a:a + size],
                                             turn[0:rows, :].rearrange("p (h c) -> p h c", h=2)[:, :, a:a + size],
                                             pT_hi[0:rows, 0:1024].rearrange("p (h c) -> p h c", h=2)[:, :, a:a + size]
                                             .bitcast(F32), ALU.subtract)
                last.then_inc(pT_set, 1)

            def gp_lo_out(u):
                dve.wait_ge(pT_hi_set, u * EVENTS + EVENTS)
                for rows, a, src in ((P, slice(0, 896), turn[:, 0:896]), (64, slice(896, 1024), turn[0:64, 896:1024]),
                                     (64, slice(1024, 1152), misc[0:64, 0:P])):
                    last = dve.tensor_tensor(pT_lo[0:rows, a], src, pT_hi[0:rows, a].bitcast(F32), ALU.subtract)
                last.then_inc(pT_set, 1)

            def inverses(u, s):
                dve.wait_ge(exp_set, u * EVENTS + s + 1)
                if s < STEPS:
                    dve.wait_ge(ctx_set, u * STEPS + s + 1)
                size = 4 if s < STEPS else 1
                dve.reciprocal(row_inv[:, 4 * s:4 * s + size], row_sum[:, 4 * s:4 * s + size]).then_inc(inv_set, 1)

            pv4 = pv[:, :].rearrange("p (g d) -> p g d", g=4)

            def pv_sums(u, s):
                dve.wait_ge(pv_lo_set, u * EVENTS + s + 1)
                dve.wait_ge(ctx_set, u * STEPS + s + STEPS - 1)
                dve.tensor_tensor(pv_sum[:, s % 2], pv4[:, :, 0:HD], pv_lo[:, :, :], ALU.add).then_inc(pv_free, 1)

            def pad_q(n, u, hp, half):
                dve.wait_ge(sel_in[half], (n + 1) * (16 * HALF_PAIRS))
                for h in range(2):
                    r = slice(h * HD, h * HD + HD)
                    last = dve.tensor_scalar(q_pad[r, r], q_sel[r, bass.ds(hp, 1), :].rearrange("p a d -> p (a d)"),
                                             HD ** -0.5, None, ALU.mult)
                last.then_inc(pad_set, 1)

            def g_out(n, u, hp):
                dve.wait_ge(pv_lo_set, u * EVENTS + EVENTS)
                dve.tensor_tensor(g_sum[0:64, :], pv4[0:64, 0, 0:HD], pv_lo[0:64, 0, :], ALU.add)
                dve.tensor_tensor(g_sum[64:P, :], pv4[64:P, 1, 0:HD], pv_lo[64:P, 0, :], ALU.add).then_inc(pv_free, 1)
                dve.wait_ge(pv_free, u * EVENTS + EVENTS + 1)
                dve.tensor_scalar(g_ctx[:, bass.ds(hp, 1), :].rearrange("p a d -> p (a d)"), g_sum[:, :],
                                  row_inv[:, 4 * STEPS:4 * STEPS + 1], None, ALU.mult).then_inc(g_set, 1)

            def attend(n, hp, half, top=(), ahead=True):
                u = n * PAIRS + hp
                tile = q_store[:, bass.ds(hp, 1), :].rearrange("p a c -> p (a c)")

                def next_rows(k):
                    if not ahead:
                        for i in LAST_TILES[k]:
                            rows_lo((n + 1) * TILES + i, ROW_ORDER[i], proj_banks)

                def top_norms(k):
                    if k < len(top):
                        top_find(n, 1, top[k])
                        if top[k] == TOP_STEPS - 1:
                            top_rows(n, 1)

                maxima(u, 0)
                v_lo_out(u, 0)
                top_norms(0)
                next_rows(0)
                v_lo_out(u, 1)
                p_lo_out(u, 0)
                maxima(u, 1)
                inverses(u, 0)
                top_norms(1)
                next_rows(1)
                v_lo_out(u, 2)
                pv_sums(u, 0)
                p_lo_out(u, 1)
                maxima(u, 2)
                inverses(u, 1)
                top_norms(2)
                next_rows(2)
                pv_sums(u, 1)
                p_lo_out(u, 2)
                maxima(u, 3)
                inverses(u, 2)
                pad_q(n, u, hp, half)
                top_norms(3)
                next_rows(3)
                pv_sums(u, 2)
                gq_lo_out(u)
                p_lo_out(u, 3)
                inverses(u, 3)
                top_norms(4)
                next_rows(4)
                global_maxima(u)
                if ahead:
                    row_moments(n, hp + 1, tile)
                pv_sums(u, 3)
                top_norms(5)
                if ahead:
                    split_q(u + 1, hp + 1)
                    k_lo_out(n, hp + 1, 0)
                next_rows(5)
                gp_lo_out(u)
                inverses(u, STEPS)
                if ahead:
                    row_roots(n, hp + 1, scale_c[:, bass.ds(hp, 1)])
                next_rows(6)
                if ahead:
                    row_normalise(tile)
                    k_lo_out(n, hp + 1, 1)
                next_rows(7)
                g_out(n, u, hp)

            for t in range(TILES):
                dve.wait_ge(first_in[t % 4], 16 * (t // 4) + 16)
                moments(q_store[:, t, :], t, last=(t == TILES - 1))
            roots(0, TILES)
            for t in range(TILES):
                normalise(q_store[:, t, :], q_store[:, t, :], t, xn_set)
                if t >= 2:
                    rows_lo(t - 2, t - 2, (proj_banks, turn_banks)[t % 2])
            for t in range(TILES - 2, TILES):
                rows_lo(t, t, (proj_banks, turn_banks)[t % 2])
            dve.wait_ge(const_in, 64)
            dve.wait_ge(pad_zero, 1)
            dve.wait_ge(base_set, 1)
            with dve.Fori(0, BATCH) as n:
                with dve.Fori(0, PAIRS // 4) as j:
                    for b, h in ((0, 0), (0, 1), (1, 0), (1, 1)):
                        norm_of(n, 2 * j + b, h)
                last_tile(n)
                for j in range(PAIRS // 4, PAIRS // 2):
                    for i, (b, h) in enumerate(((0, 0), (0, 1), (1, 0), (1, 1))):
                        norm_of(n, 2 * j + b, h)
                        r = 4 * (j - PAIRS // 4) + i
                        for step in range(3 * r, 3 * r + 3):
                            top_find(n, 0, step)
                split_q(n * PAIRS, 0)
                top_rows(n, 0)
                top_find(n, 1, 0)
                top_find(n, 1, 1)
                k_lo_out(n, 0, 0)
                top_find(n, 1, 2)
                k_lo_out(n, 0, 1)
                attend(n, 0, 0, top=range(3, 8))
                attend(n, 1, 0, top=range(8, 13))
                attend(n, 2, 0, top=range(13, 18))
                attend(n, 3, 0, top=range(18, TOP_STEPS))
                apart(dve)
                with dve.Fori(HALF_PAIRS, PAIRS - 1) as hp:
                    attend(n, hp, 1)
                attend(n, PAIRS - 1, 1, ahead=False)

            def lin_norm(t, b, turn2):
                dve.wait_ge(lin_in[b], 32 * turn2 + 32)
                if not (isinstance(t, int) and t < 2):
                    dve.wait_ge(hb_set, t - 1)
                    dve.wait_ge(lin_turned, t - 1)
                dve.tensor_tensor(lin_h[:, b, :], x_buf[:, b, :], lin_c[:, b, :], ALU.add).then_inc(h_set, 1)
                dve.wait_ge(h_set, t + 1)
                moments(lin_h[:, b, :], 0)
                roots(FIRST_STEPS + ROW_STEPS + t * LN_LINKS)
                normalise(lin_h[:, b, :], x_norm[:, b, :], 0, ln_set)

            def lin_lo(t, b):
                dve.wait_ge(lin_hi_set, t + 1)
                lo, hi = (x[b][:, :].rearrange("p (k t) -> p k t", k=KC) for x in (xlT_lo, xlT_hi))
                dve.tensor_tensor(lo, turn8, hi.bitcast(F32), ALU.subtract).then_inc(lin_set, 1)

            def lin_out(t, b, half, turn2):
                cols = slice(half * 512, half * 512 + 512)
                dve.wait_ge(lin_done[half], t + 1)
                if half == 0:
                    dve.wait_ge(hb_set, t + 1)
                    dve.wait_ge(o_stored[b], 16 * turn2 + 16)
                dve.tensor_tensor(lin_o[:, b, cols], proj[:, half, :], lin_hb[:, b, cols], ALU.add).then_inc(o_set, 1)

            lin_norm(0, 0, 0)
            lin_lo(0, 0)
            lin_norm(1, 1, 0)
            with dve.Fori(0, OUT_TILES // 2 - 1) as j:
                for b in range(2):
                    lin_out(2 * j + b, b, 0, j)
                    lin_lo(2 * j + b + 1, 1 - b)
                    lin_norm(2 * j + b + 2, b, j + 1)
                    lin_out(2 * j + b, b, 1, j)
            last = OUT_TILES // 2 - 1
            lin_out(OUT_TILES - 2, 0, 0, last)
            lin_lo(OUT_TILES - 1, 1)
            lin_out(OUT_TILES - 2, 0, 1, last)
            lin_out(OUT_TILES - 1, 1, 0, last)
            lin_out(OUT_TILES - 1, 1, 1, last)


def kernel(**inputs):
    import numpy as np
    import concourse.bacc as bacc
    from concourse.bass_utils import run_bass_kernel_spmd

    nc = bacc.Bacc("TRN2", target_bir_lowering=False, num_devices=1)

    def slices(w):
        return np.asarray(w).reshape(KC, P, PAIRS, P).transpose(2, 1, 0, 3).reshape(PAIRS, P, KC * P)

    def columns(v):
        return np.ascontiguousarray(np.asarray(v).reshape(-1, P).T)

    q, k, v = (slices(inputs[f"L0_attn_W{c}"]) for c in "qkv")
    vk = np.stack([v, k], axis=1).reshape(2 * PAIRS, P, KC * P)
    arrays = {
        "rows": np.concatenate([np.asarray(inputs["L0_attn_hidden_states"]).reshape(-1, HID),
                                np.asarray(inputs["L0_ffn_weight"])]).reshape(-1, P, HID),
        "wstream": np.concatenate([q, vk], axis=0),
        "bq": columns(inputs["L0_attn_bq"]), "bk": columns(inputs["L0_attn_bk"]), "bv": columns(inputs["L0_attn_bv"]),
        "scale_ffn": columns(inputs["L0_ffn_scale_weight"]),
        "bias_ffn": np.asarray(inputs["L0_ffn_bias"]),
    }
    given, args = {}, []
    for name, a in arrays.items():
        given[f"in_{name}"] = a = np.ascontiguousarray(a)
        args.append(nc.dram_tensor(f"in_{name}", a.shape, mybir.dt.from_np(a.dtype), kind="ExternalInput").ap())
    out = nc.dram_tensor("out", (BATCH, SEQ, HID), F32, kind="ExternalOutput").ap()
    build(nc, *args, out)
    return run_bass_kernel_spmd(nc, [given], core_ids=[0]).results[0]["out"]
```
